# Optimizing a Trainium2 kernel written in Bass

```python
import numpy as np
import jax
import jax.numpy as jnp

def _softmax(x, axis=-1):
    return jax.nn.softmax(x, axis=axis)

def _gelu(x):
    return jax.nn.gelu(x, approximate=True)

def _silu(x):
    return jax.nn.silu(x)

def _sigmoid(x):
    return jax.nn.sigmoid(x)

def _layernorm(x, axis=-1, eps=1e-05):
    m = jnp.mean(x, axis=axis, keepdims=True)
    v = jnp.var(x, axis=axis, keepdims=True)
    return (x - m) / jnp.sqrt(v + eps)

def _scatter_add(tgt, idx, src, axis=0):
    return tgt.at[idx].add(src)

def _segment_sum(src, seg, n):
    return jax.ops.segment_sum(src, seg, n)
kernel_name = 'mk_adj_preln_d1_adj_r2_ea6dc6'

def setup_inputs(seed: int=0):
    np.random.seed(seed)
    _w = jnp.asarray

    def _rec_inputs():
        import jax
        import jax.numpy as jnp
        _gk = jax.random.key(seed)
        x = 0.0002141 + 1 * jax.random.normal(jax.random.fold_in(_gk, 1), (8192, 128), jnp.float32)
        _a = jax.random.bernoulli(jax.random.fold_in(_gk, 2), 0.000488281, (8192, 8192))
        _af = _a.astype(jnp.float32)
        adj = _af
        return (x, adj)
    x, adj = _rec_inputs()

    def _L0_gnn_setup():
        import jax, jax.numpy as jnp
        import numpy as np
        N = 3072
        IN_F = 128
        OUT_F = 128
        H = 4
        OUT_PER_HEAD = OUT_F // H
        ALPHA = 0.2
        NEG_BIG = -9000000000000000.0
        key = jax.random.key(seed)
        k1, k2, k3, k4 = jax.random.split(key, 4)
        h_mat = jax.random.normal(k1, (N, IN_F), dtype=jnp.float32)
        adj = (jax.random.uniform(k2, (N, N)) < 0.05).astype(jnp.float32)
        weight = jax.random.normal(k3, (IN_F, H * OUT_PER_HEAD), dtype=jnp.float32) * (1.0 / np.sqrt(IN_F))
        att_weight = jax.random.normal(k4, (H, 2 * OUT_PER_HEAD), dtype=jnp.float32) * (1.0 / np.sqrt(OUT_PER_HEAD))
        return {'h_mat': h_mat, 'adj': adj, 'weight': weight, 'att_weight': att_weight}
    _L0_gnn_all = _L0_gnn_setup()
    _L0_gnn_in = {k: v for k, v in _L0_gnn_all.items() if k in ('weight', 'att_weight')}
    del _L0_gnn_all
    return {'x': x, 'adj': adj, 'L0_gnn_weight': _L0_gnn_in['weight'], 'L0_gnn_att_weight': _L0_gnn_in['att_weight']}

def reference(x, adj, L0_gnn_weight, L0_gnn_att_weight):
    import jax
    import jax.numpy as jnp

    def _L0_gnn_ref(h_mat, adj, weight, att_weight):
        import jax, jax.numpy as jnp
        import numpy as np
        N = 3072
        IN_F = 128
        OUT_F = 128
        H = 4
        OUT_PER_HEAD = OUT_F // H
        ALPHA = 0.2
        NEG_BIG = -9000000000000000.0
        n = h_mat.shape[0]
        wh = jnp.matmul(h_mat, weight).reshape(n, H, OUT_PER_HEAD)
        a_src = att_weight[:, :OUT_PER_HEAD]
        a_dst = att_weight[:, OUT_PER_HEAD:]
        logit_parent = jnp.einsum('nhf,hf->nh', wh, a_src)
        logit_child = jnp.einsum('nhf,hf->nh', wh, a_dst)
        e = jax.nn.leaky_relu(logit_parent[:, None, :] + logit_child[None, :, :], ALPHA)
        att = jnp.where(adj[..., None] > 0, e, NEG_BIG)
        att = jax.nn.softmax(att, axis=1)
        h_prime = jnp.einsum('njh,jhf->nhf', att, wh)
        return h_prime.reshape(n, -1)
    h = jnp.maximum(_layernorm(x, axis=-1), 0.0)
    x = x + _L0_gnn_ref(h, adj, L0_gnn_weight, L0_gnn_att_weight)
    return x

_drawn_inputs = setup_inputs


def setup_inputs(seed=0):
    import zlib

    import numpy as np

    out = dict(_drawn_inputs(seed))
    spreads = {}
    factors = {}
    for name, (base, spread) in spreads.items():
        noise = np.random.default_rng([zlib.crc32(name.encode()), seed]).standard_normal(out[name].shape)
        drawn = base * np.exp(spread * noise) if base else spread * noise
        out[name] = jnp.asarray(drawn.astype(out[name].dtype))
    for name, factor in factors.items():
        out[name] = (out[name] * factor).astype(out[name].dtype)
    return out
```

```python
from contextlib import ExitStack

import concourse.bass as bass
from concourse import mybir

ALU = mybir.AluOpType
ACT = mybir.ActivationFunctionType
AX_X = mybir.AxisListType.X
F32 = mybir.dt.float32
BF16 = mybir.dt.bfloat16
I32 = mybir.dt.int32
U32 = mybir.dt.uint32

P = 128
ALPHA = 0.2
EPS = 1e-5
FAR = 3.0e38
FLOOR = -1.0e30


def gat_kernel(nc: bass.Bass, x: bass.AP, adj: bass.AP, weight: bass.AP, att: bass.AP, out: bass.AP):
    N, D = x.shape
    H = att.shape[0]
    DH = D // H
    TILES = N // P
    BANK = 512

    CHUNK = 2048
    CHUNKS = N // CHUNK
    WORDS = 1024
    BITS = N // WORDS
    POS_BITS = 10
    assert WORDS == 1 << POS_BITS and D == P and POS_BITS + BITS < 24
    PER_CHUNK = CHUNK // WORDS
    QUARTER = 256
    FOUND = 8 * (WORDS // QUARTER)
    SLOTS = 16
    SURE = 8
    ROW = D + H
    AUG = D + 2 * H
    MEAN_ROW = N
    EXP_ONE = 127 + POS_BITS

    table = nc.dram_tensor("table", [N + 1, ROW], F32, kind="Internal").ap()
    x_rows = x.rearrange("(t p) d -> p t d", p=P)
    adj_rows = adj.rearrange("(t p) j -> p t j", p=P)
    out_rows = out.rearrange("(t p) d -> p t d", p=P)
    table_rows = table[0:N, :].rearrange("(t p) c -> p t c", p=P)

    with ExitStack() as ctx:
        def sb(name, shape, dt):
            return ctx.enter_context(nc.sbuf_tensor(name, shape, dt))

        def psum(name, shape):
            return ctx.enter_context(nc.psum_tensor(name, shape, F32))

        def sem(name):
            return ctx.enter_context(nc.semaphore(name))

        x_all = sb("x_all", [P, TILES, D], F32)
        parent = sb("parent", [P, TILES, H], F32)
        eye = sb("eye", [P, P], F32)
        eye_bits = sb("eye_bits", [P, BITS, P], BF16)
        ones_col = sb("ones_col", [P, 1], F32)
        pos_weight = sb("pos_weight", [64, P], BF16)
        pos_row = sb("pos_row", [64, WORDS], BF16)
        bit_mask = sb("bit_mask", [P, BITS], I32)
        degree_parts = sb("degree_parts", [P, TILES, CHUNKS], F32)
        counted = sb("counted", [P, TILES], F32)
        adj_ring = sb("adj_ring", [P, 2 * CHUNKS, CHUNK], F32)
        edge = [sb(f"edge{b}", [P, N], BF16) for b in range(2)]
        junk = [sb(f"junk{b}", [P, CHUNK], BF16) for b in range(2)]
        words_found = sb("words_found", [P, FOUND], I32)
        codes = sb("codes", [P, FOUND, BITS], I32)
        codes_left = sb("codes_left", [P, FOUND, BITS], I32)
        top = [sb(f"top{b}", [P, SLOTS], F32) for b in range(2)]
        used = sb("used", [P, SLOTS], F32)
        n_used = [sb(f"n_used{b}", [P, 1], F32) for b in range(2)]
        lone = sb("lone", [P, 1], F32)
        code_int = sb("code_int", [P, SLOTS], I32)
        code_exp = sb("code_exp", [P, SLOTS], I32)
        code_or = sb("code_or", [P, SLOTS], I32)
        index = [sb(f"index{b}", [P, SLOTS], I32) for b in range(2)]
        far = [sb(f"far{b}", [P, SLOTS], F32) for b in range(2)]
        most = [sb(f"most{b}", [1, 1], I32) for b in range(2)]
        near = [sb(f"near{b}", [P, SLOTS, ROW], F32) for b in range(2)]
        logit = sb("logit", [P, SLOTS, H], F32)
        row_max = sb("row_max", [P, H], F32)
        expd = sb("expd", [P, SLOTS, H], F32)
        exp_sum = sb("exp_sum", [P, H], F32)
        exp_inv = sb("exp_inv", [P, H], F32)
        share = sb("share", [P, SLOTS, H], F32)
        product = [sb(f"product{b}", [P, SLOTS, D], F32) for b in range(2)]
        out_stage = [sb(f"out_stage{b}", [P, D], F32) for b in range(2)]
        w_aug = sb("w_aug", [P, AUG], F32)
        att_all = sb("att_all", [P, H, 2, DH], F32)
        w_att = sb("w_att", [P, 2, H, DH], F32)
        stats = sb("stats", [P, TILES, 6], F32)
        mean_sum = sb("mean_sum", [P, TILES], F32)
        mean_gap = sb("mean_gap", [P, TILES], F32)
        spread = sb("spread", [P, TILES], F32)
        mean = sb("mean", [P, TILES], F32)
        var = sb("var", [P, TILES], F32)
        dev = sb("dev", [P, TILES], F32)
        rstd = sb("rstd", [P, TILES], F32)
        normed = [sb(f"normed{u}", [P, 2, D], F32) for u in range(2)]
        h_turned = [sb(f"h_turned{u}", [P, 2, P], F32) for u in range(2)]
        h_sums = sb("h_sums", [P, TILES // 2], F32)
        h_mean = sb("h_mean", [P, 1], F32)
        stage = [sb(f"stage{u}", [P, 2, ROW], F32) for u in range(2)]
        mean_stage = sb("mean_stage", [1, ROW], F32)
        short = sb("short", [P, TILES], F32)
        degree = sb("degree", [P, TILES], F32)
        flags = sb("flags", [1, TILES], I32)
        any_flag = sb("any_flag", [1, 1], I32)
        adj_block = sb("adj_block", [P, P], F32)
        table_block = sb("table_block", [P, ROW], F32)
        mean_all = sb("mean_all", [P, ROW], F32)
        not_edge = sb("not_edge", [P, P], F32)
        logits_block = product[0][:, 0:4, :]
        shares_block = product[0][:, 4:8, :]
        turned_block = product[0][:, 8:12, :]
        block_max = sb("block_max", [P, H], F32)
        block_sum = sb("block_sum", [P, H], F32)
        child_max = sb("child_max", [P, H], F32)
        redo_max = sb("redo_max", [P, H], F32)
        redo_parent = sb("redo_parent", [P, H], F32)
        redo_sum = sb("redo_sum", [P, H], F32)
        redo_inv = sb("redo_inv", [P, H], F32)
        redo_lone = sb("redo_lone", [P, 1], F32)
        redo_acc = sb("redo_acc", [P, H, DH], F32)
        redo_out = sb("redo_out", [P, D], F32)

        words = [psum(f"words{b}", [P, WORDS]) for b in range(2)]
        summed = [psum(f"summed{b}", [P, BANK]) for b in range(2)]
        small = [psum(f"small{b}", [P, BANK]) for b in range(2)]

        waits_passed = {eng.engine: sem(f"waits_passed_{k}")
                        for k, eng in enumerate((nc.vector, nc.gpsimd, nc.sync))}
        x_landed = sem("x_landed")
        weights_landed = sem("weights_landed")
        adj_landed = [sem(f"adj_landed{s}") for s in range(2 * CHUNKS)]
        eye_zero = sem("eye_zero")
        eye_made = sem("eye_made")
        pos_zero = sem("pos_zero")
        pos_made = sem("pos_made")
        eye_bits_made = sem("eye_bits_made")
        near_zero = sem("near_zero")
        masks_made = sem("masks_made")
        att_scaled = sem("att_scaled")
        w_aug_made = sem("w_aug_made")
        stats_made = sem("stats_made")
        means_made = sem("means_made")
        gap_squared = sem("gap_squared")
        var_made = sem("var_made")
        dev_made = sem("dev_made")
        rstd_made = sem("rstd_made")
        group_normed = sem("group_normed")
        group_turned = sem("group_turned")
        group_relu = sem("group_relu")
        group_projected = sem("group_projected")
        group_staged = sem("group_staged")
        group_sent = [sem(f"group_sent{u}") for u in range(2)]
        h_summed = sem("h_summed")
        h_mean_made = sem("h_mean_made")
        mean_projected = sem("mean_projected")
        mean_staged = sem("mean_staged")
        mean_sent = sem("mean_sent")
        chunk_converted = sem("chunk_converted")
        words_packed = sem("words_packed")
        degree_counted = sem("degree_counted")
        words_read = sem("words_read")
        codes_made = sem("codes_made")
        top8_made = sem("top8_made")
        top8_removed = sem("top8_removed")
        top16_made = sem("top16_made")
        used_counted = sem("used_counted")
        count_kept = sem("count_kept")
        count_turned = sem("count_turned")
        lone_made = sem("lone_made")
        top_final = sem("top_final")
        code_split = sem("code_split")
        code_joined = sem("code_joined")
        index_ready = sem("index_ready")
        most_ready = sem("most_ready")
        gathered = [sem(f"gathered{b}") for b in range(2)]
        logit_added = sem("logit_added")
        logit_leaky = sem("logit_leaky")
        logit_masked = sem("logit_masked")
        row_max_made = sem("row_max_made")
        logit_shifted = sem("logit_shifted")
        exp_made = sem("exp_made")
        exp_summed = sem("exp_summed")
        exp_inverted = sem("exp_inverted")
        share_made = sem("share_made")
        product_made = sem("product_made")
        tile_summed = sem("tile_summed")
        out_staged = sem("out_staged")
        out_sent = [sem(f"out_sent{b}") for b in range(2)]
        degree_summed = sem("degree_summed")
        short_made = sem("short_made")
        short_turned = sem("short_turned")
        flags_made = sem("flags_made")
        mean_landed = sem("mean_landed")
        block_landed = sem("block_landed")
        block_used = sem("block_used")
        child_spread = sem("child_spread")
        edges_marked = sem("edges_marked")
        child_masked = sem("child_masked")
        block_maxed = sem("block_maxed")
        redo_begun = sem("redo_begun")
        redo_max_step = sem("redo_max_step")
        pair_added = sem("pair_added")
        pair_leaky = sem("pair_leaky")
        pair_shifted = sem("pair_shifted")
        pair_masked = sem("pair_masked")
        pair_exp = sem("pair_exp")
        pair_summed = sem("pair_summed")
        pair_turned = sem("pair_turned")
        pair_copied = sem("pair_copied")
        pair_applied = sem("pair_applied")
        redo_end_step = sem("redo_end_step")
        redo_staged = sem("redo_staged")
        redo_sent = sem("redo_sent")

        def wait(eng, semaphore, value):
            if not isinstance(value, int) or value > 0:
                eng.wait_ge(semaphore, value)

        def wait_apart(eng, semaphore, value):
            if not isinstance(value, int) or value > 0:
                eng.wait_ge(semaphore, value)
                eng.sem_inc(waits_passed[eng.engine], 1)

        def one(tile):
            return bass.ds(tile, 1)

        block = ctx.enter_context(nc.Block())
        GROUPS = TILES // 2

        @block.sync
        def _(sp):
            sp.dma_start(x_all[:, 0:TILES // 2, :], x_rows[:, 0:TILES // 2, :]).then_inc(x_landed, 16)
            sp.dma_start(x_all[:, TILES // 2:, :], x_rows[:, TILES // 2:, :]).then_inc(x_landed, 16)
            sp.dma_start(w_aug[:, 0:D], weight).then_inc(weights_landed, 16)
            sp.dma_start(att_all[:].rearrange("p h s f -> p (h s f)"),
                         att.rearrange("h c -> (h c)").partition_broadcast(P)).then_inc(weights_landed, 16)

            def load_chunk(t, b, q):
                s = b * CHUNKS + q
                wait(sp, chunk_converted, (t - 2) * CHUNKS + q + 1)
                sp.dma_start(adj_ring[:, s:s + 1, :], adj_rows[:, one(t), q * CHUNK:(q + 1) * CHUNK]) \
                    .then_inc(adj_landed[s], 16)

            for b in range(2):
                for q in range(CHUNKS):
                    load_chunk(b, b, q)

            def send_group(g, u):
                sp.wait_ge(group_staged, g + 1)
                sp.dma_start(table_rows[:, bass.ds(2 * g, 2), :], stage[u][:]).then_inc(group_sent[u], 16)

            with sp.Fori(0, GROUPS // 2) as i:
                for u in range(2):
                    send_group(2 * i + u, u)
            sp.wait_ge(mean_staged, 1)
            sp.dma_start(table[MEAN_ROW:MEAN_ROW + 1, :], mean_stage[:]).then_inc(mean_sent, 16)

            with sp.Fori(1, TILES // 2) as i:
                for b in range(2):
                    for q in range(CHUNKS):
                        load_chunk(2 * i + b, b, q)

            sp.wait_ge(flags_made, 2)
            some = sp.value_load(any_flag[0:1, 0:1], min_val=0, max_val=P)
            blocks = sp.alloc_register("blocks_asked")
            redone = sp.alloc_register("tiles_redone")
            sp.reg_mov(blocks, 0)
            sp.reg_mov(redone, 0)
            for b in range(2):
                sp.wait_ge(out_sent[b], 16 * (TILES // 2))
            with sp.If(some > 0):
                sp.dma_start(mean_all[:], table[MEAN_ROW, :].partition_broadcast(P)).then_inc(mean_landed, 16)
                with sp.Fori(0, TILES) as t:
                    flag = sp.value_load(flags[0:1, one(t)], min_val=0, max_val=P)
                    with sp.If(flag > 0):
                        with sp.Fori(0, 2 * TILES) as k:
                            j = k % TILES
                            done = sp.snap(blocks, min_val=0, max_val=2 * TILES * TILES)
                            sp.wait_ge(block_used, done + 1)
                            sp.dma_start(adj_block[:].unsqueeze(1), adj_rows[:, one(t), bass.ds(j * P, P)]) \
                                .then_inc(block_landed, 16)
                            sp.dma_start(table_block[:].unsqueeze(1), table_rows[:, one(j), :]) \
                                .then_inc(block_landed, 16)
                            sp.reg_add(blocks, blocks, 1)
                        again = sp.snap(redone, min_val=0, max_val=TILES)
                        sp.wait_ge(redo_staged, again + 1)
                        sp.dma_start(out_rows[:, one(t), :], redo_out[:].unsqueeze(1)).then_inc(redo_sent, 16)
                        wait_apart(sp, redo_sent, again * 16 + 16)
                        sp.reg_add(redone, redone, 1)
                    with sp.Else():
                        sp.nop()
                    sp.nop()
                sp.nop()
            with sp.Else():
                sp.nop()
            sp.nop()

        @block.gpsimd
        def _(pool):
            nc.gpsimd.memset(eye[:], 0.0).then_inc(eye_zero, 1)
            nc.gpsimd.memset(pos_row[:], 0.0).then_inc(pos_zero, 1)
            pool.wait_ge(eye_zero, 1)
            nc.gpsimd.affine_select(out=eye[:], in_=eye[:], compare_op=ALU.not_equal, fill=1.0, base=0,
                                    pattern=[[-1, P]], channel_multiplier=1).then_inc(eye_made, 1)
            pool.wait_ge(pos_zero, 1)
            pool.wait_ge(eye_made, 1)
            nc.gpsimd.iota(pos_row[0:1, :], [[4, WORDS // 4], [0, 4]], base=0, channel_multiplier=0,
                           allow_small_or_imprecise_dtypes=True).then_inc(pos_made, 1)
            pool.wait_ge(pos_made, 1)
            nc.gpsimd.iota(pos_row[32:33, :], [[0, WORDS // 4], [1, 4]], base=0, channel_multiplier=0,
                           allow_small_or_imprecise_dtypes=True).then_inc(pos_made, 1)
            pool.wait_ge(pos_made, 2)
            for b in range(2):
                nc.gpsimd.memset(near[b][:], 0.0).then_inc(near_zero, 1)

            pool.wait_ge(near_zero, 2)
            for u in range(2):
                pool.wait_ge(group_sent[u], 16 * (GROUPS // 2))
            pool.wait_ge(mean_sent, 16)

            def gather_slot(b, s):
                pool.indirect_dma_start(near[b][:, s, :], None, table,
                                        bass.IndirectOffsetOnAxis(ap=index[b][:, s:s + 1].bitcast(U32), axis=0),
                                        bounds_check=MEAN_ROW, oob_is_err=False).then_inc(gathered[b], 16)

            def gather(t, b):
                wait_apart(pool, index_ready, t + 1)
                wait_apart(pool, product_made, t - 1)
                for s in range(SURE):
                    gather_slot(b, s)
                wait_apart(pool, most_ready, t + 1)
                longest = pool.value_load(most[b][0:1, 0:1], min_val=0, max_val=SLOTS)
                for s in range(SURE, SLOTS):
                    with pool.If(longest > s):
                        gather_slot(b, s)
                    with pool.Else():
                        pool.inc_swdge_sem([gathered[b]], [16])

            for b in range(2):
                gather(b, b)
            with pool.Fori(1, TILES // 2) as i:
                for b in range(2):
                    gather(2 * i + b, b)

        @block.scalar
        def _(act):
            act.wait_ge(var_made, 1)
            nc.scalar.activation(dev[:], var[:], ACT.Sqrt).then_inc(dev_made, 1)

            def relu_group(g, u):
                act.wait_ge(group_turned, g + 1)
                wait(act, group_projected, g - 1)
                nc.scalar.activation(h_turned[u][:].rearrange("p a d -> p (a d)"), summed[u][:, 0:2 * P], ACT.Relu,
                                     accum_out=h_sums[:, one(g)]).then_inc(group_relu, 1)

            for u in range(2):
                relu_group(u, u)
            with act.Fori(1, GROUPS // 2) as i:
                for u in range(2):
                    relu_group(2 * i + u, u)

            def count_chunk(t, b, q):
                act.wait_ge(chunk_converted, t * CHUNKS + q + 1)
                wait(act, degree_counted, t * CHUNKS + q - 1)
                nc.scalar.activation(junk[q % 2][:], edge[b][:, q * CHUNK:(q + 1) * CHUNK], ACT.Copy,
                                     accum_out=degree_parts[:, one(t), q]).then_inc(degree_counted, 1)

            def keep_count(t, b):
                act.wait_ge(used_counted, t + 1)
                nc.scalar.activation(counted[:, one(t)], n_used[b][:], ACT.Copy).then_inc(count_kept, 1)

            def exponentials(t):
                act.wait_ge(logit_shifted, t + 1)
                nc.scalar.activation(expd[:], logit[:], ACT.Exp).then_inc(exp_made, 1)

            def send_out(t, b, sent):
                act.wait_ge(tile_summed, t + 1)
                wait(act, out_sent[b], 16 * sent)
                nc.scalar.activation(out_stage[b][:], summed[b][:, 0:D], ACT.Copy).then_inc(out_staged, 1)
                act.wait_ge(out_staged, t + 1)
                act.dma_start(out_rows[:, one(t), :], out_stage[b][:].unsqueeze(1)).then_inc(out_sent[b], 16)

            def step(t, b, i, first=False, second=False, convert=True):
                if not first:
                    keep_count(t - 1, 1 - b)
                if convert:
                    for q in range(CHUNKS // 2):
                        count_chunk(t, b, q)
                if not (first or second):
                    exponentials(t - 2)
                if convert:
                    for q in range(CHUNKS // 2, CHUNKS):
                        count_chunk(t, b, q)
                if not (first or second):
                    send_out(t - 2, b, i - 1)

            step(0, 0, 0, first=True)
            step(1, 1, 0, second=True)
            for b in range(2):
                step(2 + b, b, 1)
            with act.Fori(2, TILES // 2) as i:
                for b in range(2):
                    step(2 * i + b, b, i)
            step(TILES, 0, TILES // 2, convert=False)
            exponentials(TILES - 1)
            send_out(TILES - 1, 1, TILES // 2 - 1)
            for b in range(2):
                act.wait_ge(out_sent[b], 16 * (TILES // 2))

            act.wait_ge(flags_made, 2)
            some = act.value_load(any_flag[0:1, 0:1], min_val=0, max_val=P)
            blocks = act.alloc_register("blocks_exponentiated")
            act.reg_mov(blocks, 0)
            with act.If(some > 0):
                with act.Fori(0, TILES) as t:
                    flag = act.value_load(flags[0:1, one(t)], min_val=0, max_val=P)
                    with act.If(flag > 0):
                        with act.Fori(0, TILES):
                            done = act.snap(blocks, min_val=0, max_val=TILES * TILES)
                            act.wait_ge(pair_masked, done + 1)
                            nc.scalar.activation(shares_block, logits_block, ACT.Exp).then_inc(pair_exp, 1)
                            act.reg_add(blocks, blocks, 1)
                        act.nop()
                    with act.Else():
                        act.nop()
                    act.nop()
                act.nop()
            with act.Else():
                act.nop()
            act.nop()

        @block.vector
        def _(dve):
            nc.vector.memset(ones_col[:], 1.0)
            for c in range(BITS):
                done = nc.vector.memset(bit_mask[:, c:c + 1], (1 << (POS_BITS + c)) | (WORDS - 1))
            done.then_inc(masks_made, 1)
            nc.vector.memset(pos_weight[:], 0.0).then_inc(masks_made, 1)
            dve.wait_ge(masks_made, 2)
            nc.vector.memset(pos_weight[0:1, :], 1.0)
            nc.vector.memset(pos_weight[32:33, :], 1.0).then_inc(masks_made, 1)
            dve.wait_ge(eye_made, 1)
            for c in range(BITS):
                done = nc.vector.tensor_scalar(eye_bits[:, c, :], eye[:], float(1 << (POS_BITS + c)), None, ALU.mult)
            done.then_inc(eye_bits_made, 1)

            dve.wait_ge(weights_landed, 32)
            for k, side in enumerate((1, 0)):
                nc.vector.tensor_tensor(w_att[:, k], w_aug[:, 0:D].rearrange("p (h f) -> p h f", h=H),
                                        att_all[:, :, side, :], ALU.mult).then_inc(att_scaled, 1)
            dve.wait_ge(att_scaled, 2)
            nc.vector.tensor_reduce(w_aug[:, D:AUG], w_att[:].rearrange("p k h f -> p (k h) f"), AX_X,
                                    ALU.add).then_inc(w_aug_made, 1)

            dve.wait_ge(x_landed, 32)
            with dve.Fori(0, TILES // 8) as i:
                for r in range(8):
                    nc.vector.bn_stats(stats[:, one(8 * i + r), :].squeeze(1), x_all[:, one(8 * i + r), :].squeeze(1)) \
                        .then_inc(stats_made, 1)
            dve.wait_ge(stats_made, TILES)
            nc.vector.tensor_tensor(mean_sum[:], stats[:, :, 1], stats[:, :, 4], ALU.add)
            nc.vector.tensor_tensor(mean_gap[:], stats[:, :, 1], stats[:, :, 4], ALU.subtract)
            nc.vector.tensor_tensor(spread[:], stats[:, :, 2], stats[:, :, 5], ALU.add).then_inc(means_made, 1)
            dve.wait_ge(means_made, 1)
            nc.vector.tensor_scalar(mean[:], mean_sum[:], 0.5, None, ALU.mult)
            nc.vector.scalar_tensor_tensor(mean_gap[:], mean_gap[:], 0.25, mean_gap[:], ALU.mult, ALU.mult)
            nc.vector.tensor_scalar(spread[:], spread[:], 1.0 / D, EPS, ALU.mult, ALU.add).then_inc(gap_squared, 1)
            dve.wait_ge(gap_squared, 1)
            nc.vector.tensor_tensor(var[:], spread[:], mean_gap[:], ALU.add).then_inc(var_made, 1)
            dve.wait_ge(dev_made, 1)
            nc.vector.reciprocal(rstd[:], dev[:]).then_inc(rstd_made, 1)
            dve.wait_ge(rstd_made, 1)

            def normalise(g, u):
                wait(dve, group_turned, g - 1)
                for a in range(2):
                    t = 2 * g + a
                    done = nc.vector.tensor_scalar(normed[u][:, a, :], x_all[:, one(t), :].squeeze(1),
                                                   mean[:, one(t)], rstd[:, one(t)], ALU.subtract, ALU.mult)
                done.then_inc(group_normed, 1)

            def stage_group(g, u, sent):
                dve.wait_ge(group_projected, g + 1)
                wait(dve, group_sent[u], 16 * sent)
                rows = words[u][:, 0:2 * AUG].rearrange("p (a c) -> p a c", a=2)
                nc.vector.tensor_copy(stage[u][:], rows[:, :, 0:ROW])
                nc.vector.tensor_copy(parent[:, bass.ds(2 * g, 2), :], rows[:, :, ROW:AUG]).then_inc(group_staged, 1)

            normalise(0, 0)
            normalise(1, 1)

            def stage_pair(i):
                stage_group(2 * i, 0, i)
                normalise(2 * i + 2, 0)
                stage_group(2 * i + 1, 1, i)
                normalise(2 * i + 3, 1)

            stage_pair(0)
            with dve.Fori(1, GROUPS // 2 - 1) as i:
                stage_pair(i)
            for u in range(2):
                stage_group(GROUPS - 2 + u, u, GROUPS // 2 - 1)

            dve.wait_ge(group_relu, GROUPS)
            nc.vector.tensor_reduce(h_mean[:], h_sums[:], AX_X, ALU.add).then_inc(h_summed, 1)
            dve.wait_ge(h_summed, 1)
            nc.vector.tensor_scalar(h_mean[:], h_mean[:], 1.0 / N, None, ALU.mult).then_inc(h_mean_made, 1)
            dve.wait_ge(mean_projected, 1)
            nc.vector.tensor_copy(mean_stage[:], small[0][0:1, 0:ROW]).then_inc(mean_staged, 1)

            def convert(t, b, i):
                for q in range(CHUNKS):
                    s = b * CHUNKS + q
                    dve.wait_ge(adj_landed[s], 16 * i + 16)
                    if q == 0:
                        wait(dve, words_packed, t - 1)
                        wait(dve, degree_counted, (t - 1) * CHUNKS)
                    nc.vector.tensor_scalar(edge[b][:, q * CHUNK:(q + 1) * CHUNK], adj_ring[:, s, :], 0.0, None,
                                            ALU.is_gt).then_inc(chunk_converted, 1)

            def find(t, b):
                wait_apart(dve, words_packed, t + 1)
                for f in range(WORDS // QUARTER):
                    done = nc.vector.max(words_found[:, 8 * f:8 * f + 8], words[b][:, f * QUARTER:(f + 1) * QUARTER])
                done.then_inc(words_read, 1)
                dve.wait_ge(words_read, t + 1)
                nc.vector.tensor_tensor(codes[:], words_found[:].unsqueeze(2).to_broadcast([P, FOUND, BITS]),
                                        bit_mask[:].unsqueeze(1).to_broadcast([P, FOUND, BITS]),
                                        ALU.bitwise_and).then_inc(codes_made, 1)
                wait_apart(dve, codes_made, t + 1)
                nc.vector.max(top[b][:, 0:8], codes[:]).then_inc(top8_made, 1)
                wait_apart(dve, top8_made, t + 1)
                nc.vector.match_replace(codes_left[:], top[b][:, 0:8], codes[:], 0.0).then_inc(top8_removed, 1)
                wait_apart(dve, top8_removed, t + 1)
                nc.vector.max(top[b][:, 8:16], codes_left[:]).then_inc(top16_made, 1)
                dve.wait_ge(top16_made, t + 1)
                wait(dve, count_turned, t - 1)
                wait(dve, count_kept, t - 1)
                nc.vector.tensor_scalar(used[:], top[b][:], float(WORDS), None, ALU.is_ge, ALU.add,
                                        accum_out=n_used[b][:]).then_inc(used_counted, 1)
                nc.vector.tensor_scalar(lone[:], top[b][:, 0:1], float(WORDS), float(1 << (POS_BITS + BITS)),
                                        ALU.is_lt, ALU.mult).then_inc(lone_made, 1)
                dve.wait_ge(lone_made, t + 1)
                nc.vector.tensor_tensor(top[b][:, 0:1], top[b][:, 0:1], lone[:], ALU.max).then_inc(top_final, 1)
                dve.wait_ge(top_final, t + 1)
                nc.vector.tensor_copy(code_int[:], top[b][:])
                nc.vector.tensor_scalar(code_exp[:], top[b][:].bitcast(I32), 23 - POS_BITS, 0x1FF << POS_BITS,
                                        ALU.logical_shift_right, ALU.bitwise_and)
                nc.vector.tensor_scalar(far[b][:], top[b][:], float(WORDS), -FAR, ALU.is_lt, ALU.mult) \
                    .then_inc(code_split, 1)
                dve.wait_ge(code_split, t + 1)
                nc.vector.scalar_tensor_tensor(code_or[:], code_int[:], WORDS - 1, code_exp[:], ALU.bitwise_and,
                                               ALU.bitwise_or).then_inc(code_joined, 1)
                dve.wait_ge(code_joined, t + 1)
                nc.vector.tensor_scalar(index[b][:], code_or[:], float(-(EXP_ONE << POS_BITS)), None, ALU.add) \
                    .then_inc(index_ready, 1)

            def find_longest(t, b):
                dve.wait_ge(count_turned, t + 1)
                nc.vector.tensor_reduce(most[b][:], small[b][0:1, 0:P], AX_X, ALU.max).then_inc(most_ready, 1)

            by_head = logit[:].rearrange("p s h -> p h s")

            def over_slots(per_head):
                return per_head.unsqueeze(1).to_broadcast([P, SLOTS, H])

            def attend(t, b, i):
                dve.wait_ge(gathered[b], 16 * SLOTS * i + 16 * SLOTS)
                nc.vector.tensor_tensor(logit[:], near[b][:, :, D:ROW], parent[:, one(t), :].to_broadcast([P, SLOTS, H]),
                                        ALU.add).then_inc(logit_added, 1)
                dve.wait_ge(logit_added, t + 1)
                nc.vector.scalar_tensor_tensor(logit[:], logit[:], ALPHA, logit[:], ALU.mult, ALU.max) \
                    .then_inc(logit_leaky, 1)
                dve.wait_ge(logit_leaky, t + 1)
                nc.vector.tensor_tensor(logit[:], logit[:], far[b][:].unsqueeze(2).to_broadcast([P, SLOTS, H]), ALU.add) \
                    .then_inc(logit_masked, 1)
                dve.wait_ge(logit_masked, t + 1)
                nc.vector.tensor_reduce(row_max[:], by_head, AX_X, ALU.max).then_inc(row_max_made, 1)
                dve.wait_ge(row_max_made, t + 1)
                nc.vector.tensor_tensor(logit[:], logit[:], over_slots(row_max[:]), ALU.subtract) \
                    .then_inc(logit_shifted, 1)
                dve.wait_ge(exp_made, t + 1)
                nc.vector.tensor_reduce(exp_sum[:], expd[:].rearrange("p s h -> p h s"), AX_X, ALU.add) \
                    .then_inc(exp_summed, 1)
                dve.wait_ge(exp_summed, t + 1)
                nc.vector.reciprocal(exp_inv[:], exp_sum[:]).then_inc(exp_inverted, 1)
                dve.wait_ge(exp_inverted, t + 1)
                nc.vector.tensor_tensor(share[:], expd[:], over_slots(exp_inv[:]), ALU.mult).then_inc(share_made, 1)
                dve.wait_ge(share_made, t + 1)
                wait(dve, tile_summed, t - 1)
                nc.vector.tensor_tensor(product[b][:].rearrange("p s (h f) -> p s h f", h=H),
                                        near[b][:, :, 0:D].rearrange("p s (h f) -> p s h f", h=H),
                                        share[:].unsqueeze(3).to_broadcast([P, SLOTS, H, DH]), ALU.mult) \
                    .then_inc(product_made, 1)

            def step(t, b, i, first=False, second=False, last=False):
                if not first:
                    find(t - 1, 1 - b)
                if not last:
                    convert(t, b, i)
                if not first:
                    find_longest(t - 1, 1 - b)
                if not (first or second):
                    attend(t - 2, b, i - 1)

            step(0, 0, 0, first=True)
            step(1, 1, 0, second=True)
            for b in range(2):
                step(2 + b, b, 1)
            with dve.Fori(2, TILES // 2) as i:
                for b in range(2):
                    step(2 * i + b, b, i)
            step(TILES, 0, TILES // 2, last=True)
            attend(TILES - 1, 1, TILES // 2 - 1)

            dve.wait_ge(degree_counted, TILES * CHUNKS)
            dve.wait_ge(count_kept, TILES)
            nc.vector.tensor_reduce(degree[:], degree_parts[:], AX_X, ALU.add).then_inc(degree_summed, 1)
            dve.wait_ge(degree_summed, 1)
            nc.vector.tensor_tensor(short[:], degree[:], counted[:], ALU.not_equal).then_inc(short_made, 1)
            dve.wait_ge(short_turned, 1)
            nc.vector.tensor_copy(flags[:], small[0][0:1, 0:TILES]).then_inc(flags_made, 1)
            nc.vector.tensor_reduce(any_flag[:], small[0][0:1, 0:TILES], AX_X, ALU.max).then_inc(flags_made, 1)
            dve.wait_ge(flags_made, 2)

            some = dve.value_load(any_flag[0:1, 0:1], min_val=0, max_val=P)
            blocks = dve.alloc_register("blocks_done")
            maxed = dve.alloc_register("blocks_maxed")
            rounds = dve.alloc_register("blocks_attended")
            redone = dve.alloc_register("tiles_done_again")
            dve.reg_mov(blocks, 0)
            dve.reg_mov(maxed, 0)
            dve.reg_mov(rounds, 0)
            dve.reg_mov(redone, 0)

            def mark_edges(done):
                dve.wait_ge(child_spread, done + 1)
                nc.vector.tensor_scalar(not_edge[:], adj_block[:], 0.0, 1.0, ALU.is_gt, ALU.subtract) \
                    .then_inc(edges_marked, 1)

            def off_edges():
                return not_edge[:].unsqueeze(1).to_broadcast([P, H, P])

            def over_columns(per_head):
                return per_head.unsqueeze(2).to_broadcast([P, H, P])

            spread_child = summed[0][:].rearrange("p (h j) -> p h j", h=H)
            with dve.If(some > 0):
                nc.vector.memset(block_max[:], 0.0).then_inc(block_used, 1)
                dve.wait_ge(mean_landed, 16)
                with dve.Fori(0, TILES) as t:
                    flag = dve.value_load(flags[0:1, one(t)], min_val=0, max_val=P)
                    with dve.If(flag > 0):
                        again = dve.snap(redone, min_val=0, max_val=TILES)
                        nc.vector.memset(child_max[:], -FAR)
                        nc.vector.memset(redo_sum[:], 0.0)
                        nc.vector.memset(redo_acc[:], 0.0)
                        nc.vector.tensor_copy(redo_parent[:].unsqueeze(1), parent[:, one(t), :]).then_inc(redo_begun, 1)
                        wait_apart(dve, redo_begun, again + 1)

                        with dve.Fori(0, TILES):
                            done = dve.snap(blocks, min_val=0, max_val=2 * TILES * TILES)
                            first = dve.snap(maxed, min_val=0, max_val=TILES * TILES)
                            mark_edges(done)
                            dve.wait_ge(edges_marked, done + 1)
                            nc.vector.scalar_tensor_tensor(logits_block, off_edges(), FAR, spread_child, ALU.mult,
                                                           ALU.add).then_inc(child_masked, 1)
                            dve.wait_ge(child_masked, first + 1)
                            nc.vector.tensor_reduce(block_max[:], logits_block, AX_X, ALU.max).then_inc(block_maxed, 1)
                            dve.wait_ge(block_maxed, first + 1)
                            nc.vector.tensor_tensor(child_max[:], child_max[:], block_max[:], ALU.max) \
                                .then_inc(block_used, 1)
                            wait_apart(dve, block_used, done + 2)
                            dve.reg_add(blocks, blocks, 1)
                            dve.reg_add(maxed, maxed, 1)

                        nc.vector.tensor_tensor(redo_max[:], child_max[:], redo_parent[:], ALU.add) \
                            .then_inc(redo_max_step, 1)
                        dve.wait_ge(redo_max_step, again * 3 + 1)
                        nc.vector.scalar_tensor_tensor(redo_max[:], redo_max[:], ALPHA, redo_max[:], ALU.mult, ALU.max) \
                            .then_inc(redo_max_step, 1)
                        dve.wait_ge(redo_max_step, again * 3 + 2)
                        nc.vector.tensor_scalar(redo_max[:], redo_max[:], FLOOR, None, ALU.max) \
                            .then_inc(redo_max_step, 1)
                        wait_apart(dve, redo_max_step, again * 3 + 3)

                        with dve.Fori(0, TILES):
                            done = dve.snap(blocks, min_val=0, max_val=2 * TILES * TILES)
                            second = dve.snap(rounds, min_val=0, max_val=TILES * TILES)
                            mark_edges(done)
                            nc.vector.tensor_tensor(logits_block, spread_child, over_columns(redo_parent[:]), ALU.add) \
                                .then_inc(pair_added, 1)
                            dve.wait_ge(pair_added, second + 1)
                            nc.vector.scalar_tensor_tensor(logits_block, logits_block, ALPHA, logits_block, ALU.mult,
                                                           ALU.max).then_inc(pair_leaky, 1)
                            dve.wait_ge(pair_leaky, second + 1)
                            nc.vector.tensor_tensor(logits_block, logits_block, over_columns(redo_max[:]),
                                                    ALU.subtract).then_inc(pair_shifted, 1)
                            dve.wait_ge(pair_shifted, second + 1)
                            dve.wait_ge(edges_marked, done + 1)
                            nc.vector.scalar_tensor_tensor(logits_block, off_edges(), FAR, logits_block, ALU.mult,
                                                           ALU.add).then_inc(pair_masked, 1)
                            dve.wait_ge(pair_exp, second + 1)
                            nc.vector.tensor_reduce(block_sum[:], shares_block, AX_X, ALU.add).then_inc(pair_summed, 1)
                            dve.wait_ge(pair_turned, second + 1)
                            nc.vector.tensor_copy(turned_block, summed[1][:].rearrange("p (h j) -> p h j", h=H)) \
                                .then_inc(pair_copied, 1)
                            dve.wait_ge(pair_summed, second + 1)
                            nc.vector.tensor_tensor(redo_sum[:], redo_sum[:], block_sum[:], ALU.add)
                            dve.wait_ge(pair_applied, second + 1)
                            nc.vector.tensor_tensor(redo_acc[:].rearrange("p h f -> p (h f)"),
                                                    redo_acc[:].rearrange("p h f -> p (h f)"), small[0][:, 0:D],
                                                    ALU.add).then_inc(block_used, 1)
                            wait_apart(dve, block_used, done + 2)
                            dve.reg_add(blocks, blocks, 1)
                            dve.reg_add(rounds, rounds, 1)

                        nc.vector.tensor_scalar(redo_lone[:], redo_sum[:, 0:1], 0.0, None, ALU.is_le) \
                            .then_inc(redo_end_step, 1)
                        dve.wait_ge(redo_end_step, again * 4 + 1)
                        nc.vector.tensor_scalar(redo_sum[:], redo_sum[:], redo_lone[:], None, ALU.add)
                        nc.vector.scalar_tensor_tensor(redo_acc[:].rearrange("p h f -> p (h f)"), mean_all[:, 0:D],
                                                       redo_lone[:], redo_acc[:].rearrange("p h f -> p (h f)"),
                                                       ALU.mult, ALU.add).then_inc(redo_end_step, 1)
                        dve.wait_ge(redo_end_step, again * 4 + 2)
                        nc.vector.reciprocal(redo_inv[:], redo_sum[:]).then_inc(redo_end_step, 1)
                        dve.wait_ge(redo_end_step, again * 4 + 3)
                        nc.vector.tensor_tensor(redo_acc[:], redo_acc[:],
                                                redo_inv[:].unsqueeze(2).to_broadcast([P, H, DH]), ALU.mult) \
                            .then_inc(redo_end_step, 1)
                        dve.wait_ge(redo_end_step, again * 4 + 4)
                        nc.vector.tensor_tensor(redo_out[:].unsqueeze(1),
                                                redo_acc[:].rearrange("p h f -> p (h f)").unsqueeze(1),
                                                x_all[:, one(t), :], ALU.add).then_inc(redo_staged, 1)
                        wait_apart(dve, redo_staged, again + 1)
                        dve.reg_add(redone, redone, 1)
                    with dve.Else():
                        dve.nop()
                    dve.nop()
                dve.nop()
            with dve.Else():
                dve.nop()
            dve.nop()

        @block.tensor
        def _(pe):
            def turn_group(g, u):
                pe.wait_ge(group_normed, g + 1)
                wait(pe, group_relu, g - 1)
                for a in range(2):
                    done = nc.tensor.transpose(summed[u][:, a * P:(a + 1) * P], normed[u][:, a, :], eye[:])
                done.then_inc(group_turned, 1)

            def project_group(g, u):
                pe.wait_ge(group_relu, g + 1)
                wait(pe, group_staged, g - 1)
                for a in range(2):
                    done = nc.tensor.matmul(words[u][:, a * AUG:(a + 1) * AUG], h_turned[u][:, a, :], w_aug[:],
                                            start=True, stop=True)
                done.then_inc(group_projected, 1)

            def group_pair(i):
                turn_group(2 * i + 1, 1)
                project_group(2 * i, 0)
                turn_group(2 * i + 2, 0)
                project_group(2 * i + 1, 1)

            pe.wait_ge(eye_made, 1)
            pe.wait_ge(w_aug_made, 1)
            turn_group(0, 0)
            group_pair(0)
            with pe.Fori(1, GROUPS // 2 - 1) as i:
                group_pair(i)
            turn_group(GROUPS - 1, 1)
            for u in range(2):
                project_group(GROUPS - 2 + u, u)
            pe.wait_ge(h_mean_made, 1)
            nc.tensor.matmul(small[0][0:1, 0:ROW], h_mean[:], w_aug[:, 0:ROW], start=True, stop=True) \
                .then_inc(mean_projected, 1)

            def pack(t, b):
                wait(pe, words_read, t - 1)
                for h in range(WORDS // BANK):
                    nc.tensor.matmul(words[b][:, h * BANK:(h + 1) * BANK], pos_weight[:],
                                     pos_row[:, h * BANK:(h + 1) * BANK], start=True, stop=False)
                for q in range(CHUNKS):
                    pe.wait_ge(chunk_converted, t * CHUNKS + q + 1)
                    for k in range(PER_CHUNK):
                        c = q * PER_CHUNK + k
                        for h in range(WORDS // BANK):
                            at = c * WORDS + h * BANK
                            done = nc.tensor.matmul(words[b][:, h * BANK:(h + 1) * BANK], eye_bits[:, c, :],
                                                    edge[b][:, at:at + BANK], start=False, stop=(c == BITS - 1))
                done.then_inc(words_packed, 1)

            def turn_count(t, b):
                pe.wait_ge(used_counted, t + 1)
                wait(pe, most_ready, t - 1)
                nc.tensor.matmul(small[b][0:1, 0:P], n_used[b][:], eye[:], start=True, stop=True) \
                    .then_inc(count_turned, 1)

            def add_up(t, b):
                pe.wait_ge(product_made, t + 1)
                wait(pe, out_staged, t - 1)
                nc.tensor.matmul(summed[b][:, 0:D], eye[:], x_all[:, one(t), :].squeeze(1), start=True, stop=False)
                for s in range(SLOTS):
                    done = nc.tensor.matmul(summed[b][:, 0:D], eye[:], product[b][:, s, :], start=False,
                                            stop=(s == SLOTS - 1))
                done.then_inc(tile_summed, 1)

            def step(t, b, first=False, second=False, last=False):
                if not first:
                    turn_count(t - 1, 1 - b)
                if not last:
                    pack(t, b)
                if not (first or second):
                    add_up(t - 2, b)

            pe.wait_ge(masks_made, 3)
            pe.wait_ge(pos_made, 2)
            pe.wait_ge(eye_bits_made, 1)
            pe.wait_ge(group_staged, GROUPS)
            pe.wait_ge(mean_staged, 1)
            step(0, 0, first=True)
            step(1, 1, second=True)
            for b in range(2):
                step(2 + b, b)
            with pe.Fori(2, TILES // 2) as i:
                for b in range(2):
                    step(2 * i + b, b)
            step(TILES, 0, last=True)
            add_up(TILES - 1, 1)

            pe.wait_ge(short_made, 1)
            pe.wait_ge(most_ready, TILES)
            nc.tensor.matmul(small[0][0:1, 0:TILES], ones_col[:], short[:], start=True, stop=True) \
                .then_inc(short_turned, 1)

            pe.wait_ge(flags_made, 2)
            pe.wait_ge(out_staged, TILES)
            some = pe.value_load(any_flag[0:1, 0:1], min_val=0, max_val=P)
            blocks = pe.alloc_register("blocks_seen")
            rounds = pe.alloc_register("blocks_applied")
            pe.reg_mov(blocks, 0)
            pe.reg_mov(rounds, 0)

            def spread(done):
                pe.wait_ge(block_landed, done * 32 + 32)
                for h in range(H):
                    last = nc.tensor.matmul(summed[0][:, h * P:(h + 1) * P],
                                            table_block[:, D + h:D + h + 1].to_broadcast([P, P]), eye[:],
                                            start=True, stop=True)
                last.then_inc(child_spread, 1)

            with pe.If(some > 0):
                with pe.Fori(0, TILES) as t:
                    flag = pe.value_load(flags[0:1, one(t)], min_val=0, max_val=P)
                    with pe.If(flag > 0):
                        with pe.Fori(0, TILES):
                            spread(pe.snap(blocks, min_val=0, max_val=2 * TILES * TILES))
                            pe.reg_add(blocks, blocks, 1)
                        with pe.Fori(0, TILES):
                            spread(pe.snap(blocks, min_val=0, max_val=2 * TILES * TILES))
                            second = pe.snap(rounds, min_val=0, max_val=TILES * TILES)
                            pe.wait_ge(pair_exp, second + 1)
                            for h in range(H):
                                last = nc.tensor.transpose(summed[1][:, h * P:(h + 1) * P], shares_block[:, h, :],
                                                           eye[:])
                            last.then_inc(pair_turned, 1)
                            pe.wait_ge(pair_copied, second + 1)
                            for h in range(H):
                                last = nc.tensor.matmul(small[0][:, h * DH:(h + 1) * DH], turned_block[:, h, :],
                                                        table_block[:, h * DH:(h + 1) * DH], start=True, stop=True)
                            last.then_inc(pair_applied, 1)
                            pe.reg_add(blocks, blocks, 1)
                            pe.reg_add(rounds, rounds, 1)
                        pe.nop()
                    with pe.Else():
                        pe.nop()
                    pe.nop()
                pe.nop()
            with pe.Else():
                pe.nop()
            pe.nop()


_INS = ["x", "adj", "L0_gnn_weight", "L0_gnn_att_weight"]
_OUT = ((8192, 128), "float32")


def kernel(**inputs):
    import numpy as _np
    import concourse.bacc as _bacc
    from concourse import mybir as _mybir
    from concourse.bass_utils import run_bass_kernel_spmd as _run

    nc = _bacc.Bacc("TRN2", target_bir_lowering=False, num_devices=1)
    arrays, args = {}, []
    for name in _INS:
        a = _np.ascontiguousarray(inputs[name])
        arrays[f"in_{name}_dram"] = a
        args.append(nc.dram_tensor(f"in_{name}_dram", a.shape, _mybir.dt.from_np(a.dtype), kind="ExternalInput").ap())
    shape, dtype = _OUT
    args.append(nc.dram_tensor("out_0_dram", shape, _mybir.dt.from_np(_np.dtype(dtype)), kind="ExternalOutput").ap())
    gat_kernel(nc, *args)
    r = _run(nc, [arrays], core_ids=[0])
    return r.results[0]["out_0_dram"]
```

```python
from contextlib import ExitStack

import concourse.bass as bass
from concourse import mybir

ALU = mybir.AluOpType
ACT = mybir.ActivationFunctionType
AX_X = mybir.AxisListType.X
F32 = mybir.dt.float32
BF16 = mybir.dt.bfloat16
I32 = mybir.dt.int32
U32 = mybir.dt.uint32

P = 128
ALPHA = 0.2
EPS = 1e-5
FAR = 3.0e38
FLOOR = -1.0e30


def gat_kernel(nc: bass.Bass, x: bass.AP, adj: bass.AP, weight: bass.AP, att: bass.AP, out: bass.AP):
    N, D = x.shape
    H = att.shape[0]
    DH = D // H
    TILES = N // P
    LISTS = 4
    LAG = 3
    PIECES = 4
    SET = TILES // PIECES
    GROUP = 4
    GROUPS = TILES // GROUP
    BY_VECTOR = 2
    BANK = 512

    CHUNK = 2048
    CHUNKS = N // CHUNK
    WORDS = 1024
    BITS = N // WORDS
    POS_BITS = 10
    assert WORDS == 1 << POS_BITS and D == P and POS_BITS + BITS < 24
    PER_CHUNK = CHUNK // WORDS
    QUARTER = 256
    FOUND = 8 * (WORDS // QUARTER)
    SLOTS = 16
    HALVES = (slice(0, SLOTS // 2), slice(SLOTS // 2, SLOTS))
    SURE = 8
    ROW = D + H
    assert TILES == LISTS * SLOTS
    AUG = D + 2 * H
    MEAN_ROW = N
    EXP_ONE = 127 + POS_BITS

    table = nc.dram_tensor("table", [N + 1, ROW], F32, kind="Internal").ap()
    x_rows = x.rearrange("(t p) d -> p t d", p=P)
    adj_rows = adj.rearrange("(t p) j -> p t j", p=P)
    out_rows = out.rearrange("(t p) d -> p t d", p=P)
    table_rows = table[0:N, :].rearrange("(t p) c -> p t c", p=P)

    with ExitStack() as ctx:
        def sb(name, shape, dt):
            return ctx.enter_context(nc.sbuf_tensor(name, shape, dt))

        def psum(name, shape):
            return ctx.enter_context(nc.psum_tensor(name, shape, F32))

        def sem(name):
            return ctx.enter_context(nc.semaphore(name))

        x_all = sb("x_all", [P, TILES, D], F32)
        parent = sb("parent", [P, TILES, H], F32)
        eye = sb("eye", [P, P], F32)
        eye_bits = sb("eye_bits", [P, BITS, P], BF16)
        ones_col = sb("ones_col", [P, 1], F32)
        pos_weight = sb("pos_weight", [64, P], BF16)
        pos_row = sb("pos_row", [64, WORDS], BF16)
        bit_mask = sb("bit_mask", [P, BITS], I32)
        degree_parts = sb("degree_parts", [P, TILES, CHUNKS], F32)
        counted = sb("counted", [P, TILES], F32)
        adj_ring = sb("adj_ring", [P, 2 * CHUNKS, CHUNK], F32)
        edge = [sb(f"edge{b}", [P, N], BF16) for b in range(2)]
        junk = [sb(f"junk{b}", [P, CHUNK], BF16) for b in range(2)]
        words_found = sb("words_found", [P, FOUND], I32)
        codes = sb("codes", [P, FOUND, BITS], I32)
        codes_left = sb("codes_left", [P, FOUND, BITS], I32)
        top = [sb(f"top{b}", [P, SLOTS], F32) for b in range(2)]
        used = sb("used", [P, SLOTS], F32)
        n_used = [sb(f"n_used{b}", [P, 1], F32) for b in range(2)]
        lone = sb("lone", [P, 1], F32)
        code_int = sb("code_int", [P, SLOTS], I32)
        code_exp = sb("code_exp", [P, SLOTS], I32)
        code_or = sb("code_or", [P, SLOTS], I32)
        index = [sb(f"index{k}", [P, SLOTS], I32) for k in range(LISTS)]
        far = [sb(f"far{k}", [P, SLOTS], F32) for k in range(LISTS)]
        most = [sb(f"most{k}", [1, 1], I32) for k in range(LISTS)]
        near_all = sb("near_all", [P, LISTS * SLOTS, ROW], F32)
        near = [near_all[:, k * SLOTS:(k + 1) * SLOTS, :] for k in range(LISTS)]
        logit = sb("logit", [P, SLOTS, H], F32)
        row_max = sb("row_max", [P, H], F32)
        expd = sb("expd", [P, SLOTS, H], F32)
        exp_sum = sb("exp_sum", [P, H], F32)
        exp_inv = sb("exp_inv", [P, H], F32)
        share = sb("share", [P, SLOTS, H], F32)
        product = [sb(f"product{b}", [P, SLOTS, D], F32) for b in range(2)]
        out_stage = [sb(f"out_stage{b}", [P, D], F32) for b in range(2)]
        w_aug = sb("w_aug", [P, AUG], F32)
        att_all = sb("att_all", [P, H, 2, DH], F32)
        w_att = sb("w_att", [P, 2, H, DH], F32)
        stats = sb("stats", [P, TILES, 6], F32)
        mean_sum = sb("mean_sum", [P, TILES], F32)
        mean_gap = sb("mean_gap", [P, TILES], F32)
        spread = sb("spread", [P, TILES], F32)
        mean = sb("mean", [P, TILES], F32)
        var = sb("var", [P, TILES], F32)
        dev = sb("dev", [P, TILES], F32)
        rstd = sb("rstd", [P, TILES], F32)
        shift = sb("shift", [P, TILES], F32)
        normed = [product[u][:, 0:GROUP, :] for u in range(2)]
        h_turned = [product[u][:, GROUP:2 * GROUP, :] for u in range(2)]
        h_sums = sb("h_sums", [P, GROUPS], F32)
        h_mean = sb("h_mean", [P, 1], F32)
        mean_stage = sb("mean_stage", [1, ROW], F32)
        short = sb("short", [P, TILES], F32)
        degree = sb("degree", [P, TILES], F32)
        flags = sb("flags", [1, TILES], I32)
        any_flag = sb("any_flag", [1, 1], I32)
        adj_block = sb("adj_block", [P, P], F32)
        table_block = sb("table_block", [P, ROW], F32)
        mean_all = sb("mean_all", [P, ROW], F32)
        not_edge = sb("not_edge", [P, P], F32)
        logits_block = product[0][:, 0:4, :]
        shares_block = product[0][:, 4:8, :]
        turned_block = product[0][:, 8:12, :]
        block_max = sb("block_max", [P, H], F32)
        block_sum = sb("block_sum", [P, H], F32)
        child_max = sb("child_max", [P, H], F32)
        redo_max = sb("redo_max", [P, H], F32)
        redo_parent = sb("redo_parent", [P, H], F32)
        redo_sum = sb("redo_sum", [P, H], F32)
        redo_inv = sb("redo_inv", [P, H], F32)
        redo_lone = sb("redo_lone", [P, 1], F32)
        redo_acc = sb("redo_acc", [P, H, DH], F32)
        redo_out = product[1][:, 0, :]

        words = [psum(f"words{b}", [P, WORDS]) for b in range(2)]
        summed = [psum(f"summed{b}", [P, BANK]) for b in range(2)]
        small = [psum(f"small{b}", [P, BANK]) for b in range(2)]

        waits_passed = {eng.engine: sem(f"waits_passed_{k}")
                        for k, eng in enumerate((nc.vector, nc.gpsimd, nc.sync))}
        x_landed = [sem(f"x_landed{k}") for k in range(PIECES)]
        weights_landed = sem("weights_landed")
        adj_landed = [sem(f"adj_landed{s}") for s in range(2 * CHUNKS)]
        eye_zero = sem("eye_zero")
        eye_made = sem("eye_made")
        pos_zero = sem("pos_zero")
        pos_made = sem("pos_made")
        eye_bits_made = sem("eye_bits_made")
        masks_made = sem("masks_made")
        att_scaled = sem("att_scaled")
        w_aug_made = sem("w_aug_made")
        stats_made = sem("stats_made")
        means_made = sem("means_made")
        gap_squared = sem("gap_squared")
        var_made = sem("var_made")
        dev_made = sem("dev_made")
        rstd_made = sem("rstd_made")
        shift_made = sem("shift_made")
        vector_normed = sem("vector_normed")
        scalar_normed = sem("scalar_normed")
        group_turned = sem("group_turned")
        group_relu = sem("group_relu")
        group_projected = sem("group_projected")
        group_staged = sem("group_staged")
        table_sent = sem("table_sent")
        h_summed = sem("h_summed")
        h_mean_made = sem("h_mean_made")
        mean_projected = sem("mean_projected")
        mean_staged = sem("mean_staged")
        mean_sent = sem("mean_sent")
        chunk_converted = sem("chunk_converted")
        words_packed = sem("words_packed")
        degree_counted = sem("degree_counted")
        words_read = sem("words_read")
        codes_made = sem("codes_made")
        top8_made = sem("top8_made")
        top8_removed = sem("top8_removed")
        top16_made = sem("top16_made")
        used_counted = sem("used_counted")
        count_kept = sem("count_kept")
        count_turned = sem("count_turned")
        lone_made = sem("lone_made")
        top_final = sem("top_final")
        code_split = sem("code_split")
        code_joined = sem("code_joined")
        index_ready = sem("index_ready")
        most_ready = sem("most_ready")
        gathered = [sem(f"gathered{k}") for k in range(LISTS)]
        logit_added = sem("logit_added")
        logit_leaky = sem("logit_leaky")
        logit_masked = sem("logit_masked")
        row_max_made = sem("row_max_made")
        logit_shifted = sem("logit_shifted")
        exp_made = sem("exp_made")
        exp_summed = sem("exp_summed")
        exp_inverted = sem("exp_inverted")
        share_made = sem("share_made")
        product_made = sem("product_made")
        tile_summed = sem("tile_summed")
        out_staged = sem("out_staged")
        out_sent = [sem(f"out_sent{b}") for b in range(2)]
        degree_summed = sem("degree_summed")
        short_made = sem("short_made")
        short_turned = sem("short_turned")
        flags_made = sem("flags_made")
        mean_landed = sem("mean_landed")
        block_landed = sem("block_landed")
        block_used = sem("block_used")
        child_spread = sem("child_spread")
        edges_marked = sem("edges_marked")
        child_masked = sem("child_masked")
        block_maxed = sem("block_maxed")
        redo_begun = sem("redo_begun")
        redo_max_step = sem("redo_max_step")
        pair_added = sem("pair_added")
        pair_leaky = sem("pair_leaky")
        pair_shifted = sem("pair_shifted")
        pair_masked = sem("pair_masked")
        pair_exp = sem("pair_exp")
        pair_summed = sem("pair_summed")
        pair_turned = sem("pair_turned")
        pair_copied = sem("pair_copied")
        pair_applied = sem("pair_applied")
        redo_end_step = sem("redo_end_step")
        redo_staged = sem("redo_staged")
        redo_sent = sem("redo_sent")

        def wait(eng, semaphore, value):
            if not isinstance(value, int) or value > 0:
                eng.wait_ge(semaphore, value)

        def wait_apart(eng, semaphore, value):
            if not isinstance(value, int) or value > 0:
                eng.wait_ge(semaphore, value)
                eng.sem_inc(waits_passed[eng.engine], 1)

        def one(tile):
            return bass.ds(tile, 1)

        def at(i, r, lag=0):
            return LISTS * i + r - lag, (r - lag) % LISTS, i + (r - lag) // LISTS

        def is_tile(t):
            return not isinstance(t, int) or 0 <= t < TILES

        def every_step(eng, step):
            for i in range(2):
                for r in range(LISTS):
                    step(i, r)
            with eng.Fori(2, TILES // LISTS) as i:
                for r in range(LISTS):
                    step(i, r)
            for r in range(LISTS):
                step(TILES // LISTS, r)

        def projected(u):
            return words[u][:].rearrange("p (k r) -> p k r", k=2)[:, :, 0:2 * AUG] \
                .rearrange("p k (a c) -> p k a c", a=2)

        block = ctx.enter_context(nc.Block())

        @block.sync
        def _(sp):
            sp.dma_start(w_aug[:, 0:D], weight).then_inc(weights_landed, 16)
            sp.dma_start(att_all[:].rearrange("p h s f -> p (h s f)"),
                         att.rearrange("h c -> (h c)").partition_broadcast(P)).then_inc(weights_landed, 16)
            for k in range(PIECES):
                sp.dma_start(x_all[:, k * SET:(k + 1) * SET, :], x_rows[:, k * SET:(k + 1) * SET, :]) \
                    .then_inc(x_landed[k], 16)

            def load_tile(t, b):
                for q in range(CHUNKS):
                    s = b * CHUNKS + q
                    wait(sp, chunk_converted, (t - 2) * CHUNKS + q + 1)
                    sp.dma_start(adj_ring[:, s:s + 1, :], adj_rows[:, one(t), q * CHUNK:(q + 1) * CHUNK]) \
                        .then_inc(adj_landed[s], 16)

            load_tile(0, 0)
            load_tile(1, 1)
            for k in range(PIECES):
                if k == 1:
                    load_tile(2, 0)
                sp.wait_ge(group_staged, SET // GROUP * (k + 1))
                sp.dma_start(table_rows[:, k * SET:(k + 1) * SET, :], near_all[:, k * SET:(k + 1) * SET, :]) \
                    .then_inc(table_sent, 16)
            sp.wait_ge(mean_staged, 1)
            sp.dma_start(table[MEAN_ROW:MEAN_ROW + 1, :], mean_stage[:]).then_inc(mean_sent, 16)
            load_tile(3, 1)
            with sp.Fori(2, TILES // 2) as i:
                for b in range(2):
                    load_tile(2 * i + b, b)

            sp.wait_ge(flags_made, 2)
            some = sp.value_load(any_flag[0:1, 0:1], min_val=0, max_val=P)
            blocks = sp.alloc_register("blocks_asked")
            redone = sp.alloc_register("tiles_redone")
            sp.reg_mov(blocks, 0)
            sp.reg_mov(redone, 0)
            for b in range(2):
                sp.wait_ge(out_sent[b], 16 * (TILES // 2))
            with sp.If(some > 0):
                sp.dma_start(mean_all[:], table[MEAN_ROW, :].partition_broadcast(P)).then_inc(mean_landed, 16)
                with sp.Fori(0, TILES) as t:
                    flag = sp.value_load(flags[0:1, one(t)], min_val=0, max_val=P)
                    with sp.If(flag > 0):
                        with sp.Fori(0, 2 * TILES) as k:
                            j = k % TILES
                            done = sp.snap(blocks, min_val=0, max_val=2 * TILES * TILES)
                            sp.wait_ge(block_used, done + 1)
                            sp.dma_start(adj_block[:].unsqueeze(1), adj_rows[:, one(t), bass.ds(j * P, P)]) \
                                .then_inc(block_landed, 16)
                            sp.dma_start(table_block[:].unsqueeze(1), table_rows[:, one(j), :]) \
                                .then_inc(block_landed, 16)
                            sp.reg_add(blocks, blocks, 1)
                        again = sp.snap(redone, min_val=0, max_val=TILES)
                        sp.wait_ge(redo_staged, again + 1)
                        sp.dma_start(out_rows[:, one(t), :], redo_out.unsqueeze(1)).then_inc(redo_sent, 16)
                        wait_apart(sp, redo_sent, again * 16 + 16)
                        sp.reg_add(redone, redone, 1)
                    with sp.Else():
                        sp.nop()
                    sp.nop()
                sp.nop()
            with sp.Else():
                sp.nop()
            sp.nop()

        @block.gpsimd
        def _(pool):
            nc.gpsimd.memset(eye[:], 0.0).then_inc(eye_zero, 1)
            nc.gpsimd.memset(pos_row[:], 0.0).then_inc(pos_zero, 1)
            pool.wait_ge(eye_zero, 1)
            nc.gpsimd.affine_select(out=eye[:], in_=eye[:], compare_op=ALU.not_equal, fill=1.0, base=0,
                                    pattern=[[-1, P]], channel_multiplier=1).then_inc(eye_made, 1)
            pool.wait_ge(pos_zero, 1)
            pool.wait_ge(eye_made, 1)
            nc.gpsimd.iota(pos_row[0:1, :], [[4, WORDS // 4], [0, 4]], base=0, channel_multiplier=0,
                           allow_small_or_imprecise_dtypes=True).then_inc(pos_made, 1)
            pool.wait_ge(pos_made, 1)
            nc.gpsimd.iota(pos_row[32:33, :], [[0, WORDS // 4], [1, 4]], base=0, channel_multiplier=0,
                           allow_small_or_imprecise_dtypes=True).then_inc(pos_made, 1)
            pool.wait_ge(pos_made, 2)

            pool.wait_ge(table_sent, 16 * PIECES)
            pool.wait_ge(mean_sent, 16)

            def gather_slot(k, s):
                pool.indirect_dma_start(near[k][:, s, :], None, table,
                                        bass.IndirectOffsetOnAxis(ap=index[k][:, s:s + 1].bitcast(U32), axis=0),
                                        bounds_check=MEAN_ROW, oob_is_err=False).then_inc(gathered[k], 16)

            def gather(i, r):
                t, k, _ = at(i, r)
                wait_apart(pool, index_ready, t + 1)
                wait_apart(pool, product_made, 2 * (t - LISTS + 1))
                for s in range(SURE):
                    gather_slot(k, s)
                wait_apart(pool, most_ready, t + 1)
                longest = pool.value_load(most[k][0:1, 0:1], min_val=0, max_val=SLOTS)
                for s in range(SURE, SLOTS):
                    with pool.If(longest > s):
                        gather_slot(k, s)
                    with pool.Else():
                        pool.inc_swdge_sem([gathered[k]], [16])

            for r in range(LISTS):
                gather(0, r)
            with pool.Fori(1, TILES // LISTS) as i:
                for r in range(LISTS):
                    gather(i, r)

        @block.scalar
        def _(act):
            def deviation(k):
                act.wait_ge(var_made, k + 1)
                nc.scalar.activation(dev[:, k * SET:(k + 1) * SET], var[:, k * SET:(k + 1) * SET], ACT.Sqrt) \
                    .then_inc(dev_made, 1)

            def normalise(g, u):
                wait(act, group_turned, g - 1)
                for a in range(BY_VECTOR, GROUP):
                    t = GROUP * g + a
                    done = nc.scalar.activation(normed[u][:, a, :], x_all[:, one(t), :].squeeze(1), ACT.Identity,
                                                bias=shift[:, one(t)], scale=rstd[:, one(t)])
                done.then_inc(scalar_normed, 1)

            def relu_group(g, u):
                act.wait_ge(group_turned, g + 1)
                wait(act, group_projected, g - 1)
                nc.scalar.activation(h_turned[u].rearrange("p a d -> p (a d)"), summed[u][:], ACT.Relu,
                                     accum_out=h_sums[:, one(g)]).then_inc(group_relu, 1)

            def stage_group(g, u):
                act.wait_ge(group_projected, g + 1)
                nc.scalar.activation(near_all[:, bass.ds(GROUP * g, GROUP), :].rearrange("p (k a) c -> p k a c", k=2), projected(u)[:, :, :, 0:ROW],
                                     ACT.Copy)
                nc.scalar.activation(parent[:, bass.ds(GROUP * g, GROUP), :].rearrange("p (k a) h -> p k a h", k=2),
                                     projected(u)[:, :, :, ROW:AUG], ACT.Copy).then_inc(group_staged, 1)

            def group_pair(i, last=False):
                relu_group(2 * i + 1, 1)
                normalise(2 * i + 3, 1)
                stage_group(2 * i, 0)
                relu_group(2 * i + 2, 0)
                if not last:
                    normalise(2 * i + 4, 0)
                stage_group(2 * i + 1, 1)

            deviation(0)
            act.wait_ge(shift_made, 1)
            normalise(0, 0)
            normalise(1, 1)
            relu_group(0, 0)
            normalise(2, 0)
            for k in range(1, PIECES):
                deviation(k)
                act.wait_ge(shift_made, k + 1)
                for i in range(2 * k - 2, 2 * k) if k == 1 else ():
                    group_pair(i)
                if k > 1:
                    with act.Fori(2 * k - 2, 2 * k) as i:
                        group_pair(i)
            group_pair(GROUPS // 2 - 2, last=True)
            relu_group(GROUPS - 1, 1)
            for u in range(2):
                stage_group(GROUPS - 2 + u, u)

            def count_chunk(t, b, q):
                act.wait_ge(chunk_converted, t * CHUNKS + q + 1)
                wait(act, degree_counted, t * CHUNKS + q - 1)
                nc.scalar.activation(junk[q % 2][:], edge[b][:, q * CHUNK:(q + 1) * CHUNK], ACT.Copy,
                                     accum_out=degree_parts[:, one(t), q]).then_inc(degree_counted, 1)

            def keep_count(t, b):
                act.wait_ge(used_counted, t + 1)
                nc.scalar.activation(counted[:, one(t)], n_used[b][:], ACT.Copy).then_inc(count_kept, 1)

            def exponentials(t):
                act.wait_ge(logit_shifted, t + 1)
                nc.scalar.activation(expd[:], logit[:], ACT.Exp).then_inc(exp_made, 1)

            def send_out(t, b, before):
                act.wait_ge(tile_summed, t + 1)
                wait(act, out_sent[b], 16 * before)
                nc.scalar.activation(out_stage[b][:], summed[b][:, 0:D], ACT.Copy).then_inc(out_staged, 1)
                act.wait_ge(out_staged, t + 1)
                act.dma_start(out_rows[:, one(t), :], out_stage[b][:].unsqueeze(1)).then_inc(out_sent[b], 16)

            def step(i, r):
                t, k, _ = at(i, r, LAG)
                if is_tile(t):
                    exponentials(t)
                t, k, _ = at(i, r, 1)
                if is_tile(t):
                    keep_count(t, k % 2)
                    for q in range(CHUNKS):
                        count_chunk(t, k % 2, q)
                t, k, n = at(i, r, LAG + 1)
                if is_tile(t):
                    send_out(t, k % 2, 2 * n + k // 2)

            every_step(act, step)
            for b in range(2):
                act.wait_ge(out_sent[b], 16 * (TILES // 2))

            act.wait_ge(flags_made, 2)
            some = act.value_load(any_flag[0:1, 0:1], min_val=0, max_val=P)
            blocks = act.alloc_register("blocks_exponentiated")
            act.reg_mov(blocks, 0)
            with act.If(some > 0):
                with act.Fori(0, TILES) as t:
                    flag = act.value_load(flags[0:1, one(t)], min_val=0, max_val=P)
                    with act.If(flag > 0):
                        with act.Fori(0, TILES):
                            done = act.snap(blocks, min_val=0, max_val=TILES * TILES)
                            act.wait_ge(pair_masked, done + 1)
                            nc.scalar.activation(shares_block, logits_block, ACT.Exp).then_inc(pair_exp, 1)
                            act.reg_add(blocks, blocks, 1)
                        act.nop()
                    with act.Else():
                        act.nop()
                    act.nop()
                act.nop()
            with act.Else():
                act.nop()
            act.nop()

        @block.vector
        def _(dve):
            nc.vector.memset(ones_col[:], 1.0)
            for c in range(BITS):
                done = nc.vector.memset(bit_mask[:, c:c + 1], (1 << (POS_BITS + c)) | (WORDS - 1))
            done.then_inc(masks_made, 1)
            nc.vector.memset(pos_weight[:], 0.0).then_inc(masks_made, 1)
            dve.wait_ge(masks_made, 2)
            nc.vector.memset(pos_weight[0:1, :], 1.0)
            nc.vector.memset(pos_weight[32:33, :], 1.0).then_inc(masks_made, 1)
            dve.wait_ge(eye_made, 1)
            for c in range(BITS):
                done = nc.vector.tensor_scalar(eye_bits[:, c, :], eye[:], float(1 << (POS_BITS + c)), None, ALU.mult)
            done.then_inc(eye_bits_made, 1)

            dve.wait_ge(weights_landed, 32)
            for k, side in enumerate((1, 0)):
                nc.vector.tensor_tensor(w_att[:, k], w_aug[:, 0:D].rearrange("p (h f) -> p h f", h=H),
                                        att_all[:, :, side, :], ALU.mult).then_inc(att_scaled, 1)
            dve.wait_ge(att_scaled, 2)
            nc.vector.tensor_reduce(w_aug[:, D:AUG], w_att[:].rearrange("p k h f -> p (k h) f"), AX_X,
                                    ALU.add).then_inc(w_aug_made, 1)

            def row_stats(k):
                dve.wait_ge(x_landed[k], 16)
                with dve.Fori(k * SET // 8, (k + 1) * SET // 8) as i:
                    for r in range(8):
                        nc.vector.bn_stats(stats[:, one(8 * i + r), :].squeeze(1),
                                           x_all[:, one(8 * i + r), :].squeeze(1)).then_inc(stats_made, 1)

            def row_variances(k):
                of = slice(k * SET, (k + 1) * SET)
                dve.wait_ge(stats_made, (k + 1) * SET)
                nc.vector.tensor_tensor(mean_sum[:, of], stats[:, of, 1], stats[:, of, 4], ALU.add)
                nc.vector.tensor_tensor(mean_gap[:, of], stats[:, of, 1], stats[:, of, 4], ALU.subtract)
                nc.vector.tensor_tensor(spread[:, of], stats[:, of, 2], stats[:, of, 5], ALU.add) \
                    .then_inc(means_made, 1)
                dve.wait_ge(means_made, k + 1)
                nc.vector.tensor_scalar(mean[:, of], mean_sum[:, of], 0.5, None, ALU.mult)
                nc.vector.scalar_tensor_tensor(mean_gap[:, of], mean_gap[:, of], 0.25, mean_gap[:, of], ALU.mult,
                                               ALU.mult)
                nc.vector.tensor_scalar(spread[:, of], spread[:, of], 1.0 / D, EPS, ALU.mult, ALU.add) \
                    .then_inc(gap_squared, 1)
                dve.wait_ge(gap_squared, k + 1)
                nc.vector.tensor_tensor(var[:, of], spread[:, of], mean_gap[:, of], ALU.add).then_inc(var_made, 1)

            def row_scales(k):
                of = slice(k * SET, (k + 1) * SET)
                dve.wait_ge(dev_made, k + 1)
                nc.vector.reciprocal(rstd[:, of], dev[:, of]).then_inc(rstd_made, 1)
                dve.wait_ge(rstd_made, k + 1)
                nc.vector.scalar_tensor_tensor(shift[:, of], mean[:, of], -1.0, rstd[:, of], ALU.mult, ALU.mult) \
                    .then_inc(shift_made, 1)

            def normalise(g, u):
                wait(dve, group_turned, g - 1)
                for a in range(BY_VECTOR):
                    t = GROUP * g + a
                    done = nc.vector.tensor_scalar(normed[u][:, a, :], x_all[:, one(t), :].squeeze(1),
                                                   mean[:, one(t)], rstd[:, one(t)], ALU.subtract, ALU.mult)
                done.then_inc(vector_normed, 1)

            def convert(t, b, before, chunks):
                for q in chunks:
                    s = b * CHUNKS + q
                    dve.wait_ge(adj_landed[s], 16 * before + 16)
                    if q == 0:
                        wait(dve, words_packed, t - 1)
                        wait(dve, degree_counted, (t - 1) * CHUNKS)
                    nc.vector.tensor_scalar(edge[b][:, q * CHUNK:(q + 1) * CHUNK], adj_ring[:, s, :], 0.0, None,
                                            ALU.is_gt).then_inc(chunk_converted, 1)

            for k in range(PIECES + 1):
                if k < PIECES:
                    row_stats(k)
                    row_variances(k)
                if k == 1:
                    dve.wait_ge(shift_made, k)
                    normalise(0, 0)
                    normalise(1, 1)
                if k > 0:
                    dve.wait_ge(shift_made, k)
                    with dve.Fori(max(1, (k - 1) * SET // GROUP // 2), k * SET // GROUP // 2) as i:
                        for u in range(2):
                            normalise(2 * i + u, u)
                if k < PIECES:
                    row_scales(k)
                if k in (2, 3):
                    convert(0, 0, 0, range(2 * k - 4, 2 * k - 2))

            dve.wait_ge(group_relu, GROUPS)
            nc.vector.tensor_reduce(h_mean[:], h_sums[:], AX_X, ALU.add).then_inc(h_summed, 1)
            dve.wait_ge(h_summed, 1)
            nc.vector.tensor_scalar(h_mean[:], h_mean[:], 1.0 / N, None, ALU.mult).then_inc(h_mean_made, 1)
            dve.wait_ge(mean_projected, 1)
            nc.vector.tensor_copy(mean_stage[:], small[0][0:1, 0:ROW]).then_inc(mean_staged, 1)
            convert(1, 1, 0, range(CHUNKS))

            def find_words(t, b):
                wait_apart(dve, words_packed, t + 1)
                for f in range(WORDS // QUARTER):
                    done = nc.vector.max(words_found[:, 8 * f:8 * f + 8], words[b][:, f * QUARTER:(f + 1) * QUARTER])
                done.then_inc(words_read, 1)

            def find_codes(t):
                dve.wait_ge(words_read, t + 1)
                nc.vector.tensor_tensor(codes[:], words_found[:].unsqueeze(2).to_broadcast([P, FOUND, BITS]),
                                        bit_mask[:].unsqueeze(1).to_broadcast([P, FOUND, BITS]),
                                        ALU.bitwise_and).then_inc(codes_made, 1)

            def find_first8(t, b):
                wait_apart(dve, codes_made, t + 1)
                nc.vector.max(top[b][:, 0:8], codes[:]).then_inc(top8_made, 1)

            def remove_first8(t, b):
                wait_apart(dve, top8_made, t + 1)
                nc.vector.match_replace(codes_left[:], top[b][:, 0:8], codes[:], 0.0).then_inc(top8_removed, 1)

            def find_next8(t, b):
                wait_apart(dve, top8_removed, t + 1)
                nc.vector.max(top[b][:, 8:16], codes_left[:]).then_inc(top16_made, 1)

            def count_used(t, b):
                dve.wait_ge(top16_made, t + 1)
                wait(dve, count_turned, t - 1)
                wait(dve, count_kept, t - 1)
                nc.vector.tensor_scalar(used[:], top[b][:], float(WORDS), None, ALU.is_ge, ALU.add,
                                        accum_out=n_used[b][:]).then_inc(used_counted, 1)
                nc.vector.tensor_scalar(lone[:], top[b][:, 0:1], float(WORDS), float(1 << (POS_BITS + BITS)),
                                        ALU.is_lt, ALU.mult).then_inc(lone_made, 1)

            def place_lone(t, b):
                dve.wait_ge(lone_made, t + 1)
                nc.vector.tensor_tensor(top[b][:, 0:1], top[b][:, 0:1], lone[:], ALU.max).then_inc(top_final, 1)

            def split_codes(t, b, k):
                dve.wait_ge(top_final, t + 1)
                nc.vector.tensor_copy(code_int[:], top[b][:])
                nc.vector.tensor_scalar(code_exp[:], top[b][:].bitcast(I32), 23 - POS_BITS, 0x1FF << POS_BITS,
                                        ALU.logical_shift_right, ALU.bitwise_and)
                nc.vector.tensor_scalar(far[k][:], top[b][:], float(WORDS), -FAR, ALU.is_lt, ALU.mult) \
                    .then_inc(code_split, 1)

            def join_codes(t):
                dve.wait_ge(code_split, t + 1)
                nc.vector.scalar_tensor_tensor(code_or[:], code_int[:], WORDS - 1, code_exp[:], ALU.bitwise_and,
                                               ALU.bitwise_or).then_inc(code_joined, 1)

            def make_index(t, k):
                dve.wait_ge(code_joined, t + 1)
                nc.vector.tensor_scalar(index[k][:], code_or[:], float(-(EXP_ONE << POS_BITS)), None, ALU.add) \
                    .then_inc(index_ready, 1)

            def find_longest(t, b, k):
                dve.wait_ge(count_turned, t + 1)
                nc.vector.tensor_reduce(most[k][:], small[b][0:1, 0:P], AX_X, ALU.max).then_inc(most_ready, 1)

            def over_slots(per_head):
                return per_head.unsqueeze(1).to_broadcast([P, SLOTS, H])

            def add_logits(t, k, before):
                dve.wait_ge(gathered[k], 16 * SLOTS * before + 16 * SLOTS)
                nc.vector.tensor_tensor(logit[:], near[k][:, :, D:ROW], parent[:, one(t), :].to_broadcast([P, SLOTS, H]),
                                        ALU.add).then_inc(logit_added, 1)

            def leak_logits(t):
                dve.wait_ge(logit_added, t + 1)
                nc.vector.scalar_tensor_tensor(logit[:], logit[:], ALPHA, logit[:], ALU.mult, ALU.max) \
                    .then_inc(logit_leaky, 1)

            def mask_logits(t, k):
                dve.wait_ge(logit_leaky, t + 1)
                nc.vector.tensor_tensor(logit[:], logit[:], far[k][:].unsqueeze(2).to_broadcast([P, SLOTS, H]),
                                        ALU.add).then_inc(logit_masked, 1)

            def find_max(t):
                dve.wait_ge(logit_masked, t + 1)
                nc.vector.tensor_reduce(row_max[:], logit[:].rearrange("p s h -> p h s"), AX_X, ALU.max) \
                    .then_inc(row_max_made, 1)

            def shift_logits(t):
                dve.wait_ge(row_max_made, t + 1)
                nc.vector.tensor_tensor(logit[:], logit[:], over_slots(row_max[:]), ALU.subtract) \
                    .then_inc(logit_shifted, 1)

            def sum_exps(t):
                dve.wait_ge(exp_made, t + 1)
                nc.vector.tensor_reduce(exp_sum[:], expd[:].rearrange("p s h -> p h s"), AX_X, ALU.add) \
                    .then_inc(exp_summed, 1)

            def invert_sums(t):
                dve.wait_ge(exp_summed, t + 1)
                nc.vector.reciprocal(exp_inv[:], exp_sum[:]).then_inc(exp_inverted, 1)

            def make_shares(t):
                dve.wait_ge(exp_inverted, t + 1)
                nc.vector.tensor_tensor(share[:], expd[:], over_slots(exp_inv[:]), ALU.mult).then_inc(share_made, 1)

            def multiply(t, k):
                b = k % 2
                dve.wait_ge(share_made, t + 1)
                wait(dve, tile_summed, t - 1)
                for of in HALVES:
                    nc.vector.tensor_tensor(product[b][:, of, :].rearrange("p s (h f) -> p s h f", h=H),
                                            near[k][:, of, 0:D].rearrange("p s (h f) -> p s h f", h=H),
                                            share[:, of, :].unsqueeze(3).to_broadcast([P, SLOTS // 2, H, DH]),
                                            ALU.mult).then_inc(product_made, 1)

            def step(i, r):
                t, k, n = at(i, r)
                found, fk, _ = at(i, r, 1)
                summed_up, sk, before = at(i, r, LAG)
                b, fb = k % 2, fk % 2
                converting = is_tile(t) and not (isinstance(t, int) and t < 2)
                finding, attending = is_tile(found), is_tile(summed_up)
                if finding:
                    find_words(found, fb)
                if attending:
                    add_logits(summed_up, sk, before)
                if finding:
                    find_codes(found)
                if attending:
                    leak_logits(summed_up)
                if finding:
                    find_first8(found, fb)
                if attending:
                    mask_logits(summed_up, sk)
                if finding:
                    remove_first8(found, fb)
                if attending:
                    find_max(summed_up)
                if finding:
                    find_next8(found, fb)
                if attending:
                    shift_logits(summed_up)
                if finding:
                    count_used(found, fb)
                if converting:
                    convert(t, b, 2 * n + k // 2, range(0, 1))
                if finding:
                    place_lone(found, fb)
                if attending:
                    sum_exps(summed_up)
                if finding:
                    split_codes(found, fb, fk)
                if attending:
                    invert_sums(summed_up)
                if finding:
                    join_codes(found)
                if attending:
                    make_shares(summed_up)
                if finding:
                    make_index(found, fk)
                if converting:
                    convert(t, b, 2 * n + k // 2, range(1, 2))
                if attending:
                    multiply(summed_up, sk)
                if converting:
                    convert(t, b, 2 * n + k // 2, range(2, 3))
                if finding:
                    find_longest(found, fb, fk)
                if converting:
                    convert(t, b, 2 * n + k // 2, range(3, CHUNKS))

            every_step(dve, step)

            dve.wait_ge(degree_counted, TILES * CHUNKS)
            dve.wait_ge(count_kept, TILES)
            nc.vector.tensor_reduce(degree[:], degree_parts[:], AX_X, ALU.add).then_inc(degree_summed, 1)
            dve.wait_ge(degree_summed, 1)
            nc.vector.tensor_tensor(short[:], degree[:], counted[:], ALU.not_equal).then_inc(short_made, 1)
            dve.wait_ge(short_turned, 1)
            nc.vector.tensor_copy(flags[:], small[0][0:1, 0:TILES]).then_inc(flags_made, 1)
            nc.vector.tensor_reduce(any_flag[:], small[0][0:1, 0:TILES], AX_X, ALU.max).then_inc(flags_made, 1)
            dve.wait_ge(flags_made, 2)

            some = dve.value_load(any_flag[0:1, 0:1], min_val=0, max_val=P)
            blocks = dve.alloc_register("blocks_done")
            maxed = dve.alloc_register("blocks_maxed")
            rounds = dve.alloc_register("blocks_attended")
            redone = dve.alloc_register("tiles_done_again")
            dve.reg_mov(blocks, 0)
            dve.reg_mov(maxed, 0)
            dve.reg_mov(rounds, 0)
            dve.reg_mov(redone, 0)

            def mark_edges(done):
                dve.wait_ge(child_spread, done + 1)
                nc.vector.tensor_scalar(not_edge[:], adj_block[:], 0.0, 1.0, ALU.is_gt, ALU.subtract) \
                    .then_inc(edges_marked, 1)

            def off_edges():
                return not_edge[:].unsqueeze(1).to_broadcast([P, H, P])

            def over_columns(per_head):
                return per_head.unsqueeze(2).to_broadcast([P, H, P])

            spread_child = summed[0][:].rearrange("p (h j) -> p h j", h=H)
            with dve.If(some > 0):
                nc.vector.memset(block_max[:], 0.0).then_inc(block_used, 1)
                dve.wait_ge(mean_landed, 16)
                with dve.Fori(0, TILES) as t:
                    flag = dve.value_load(flags[0:1, one(t)], min_val=0, max_val=P)
                    with dve.If(flag > 0):
                        again = dve.snap(redone, min_val=0, max_val=TILES)
                        nc.vector.memset(child_max[:], -FAR)
                        nc.vector.memset(redo_sum[:], 0.0)
                        nc.vector.memset(redo_acc[:], 0.0)
                        nc.vector.tensor_copy(redo_parent[:].unsqueeze(1), parent[:, one(t), :]).then_inc(redo_begun, 1)
                        wait_apart(dve, redo_begun, again + 1)

                        with dve.Fori(0, TILES):
                            done = dve.snap(blocks, min_val=0, max_val=2 * TILES * TILES)
                            first = dve.snap(maxed, min_val=0, max_val=TILES * TILES)
                            mark_edges(done)
                            dve.wait_ge(edges_marked, done + 1)
                            nc.vector.scalar_tensor_tensor(logits_block, off_edges(), FAR, spread_child, ALU.mult,
                                                           ALU.add).then_inc(child_masked, 1)
                            dve.wait_ge(child_masked, first + 1)
                            nc.vector.tensor_reduce(block_max[:], logits_block, AX_X, ALU.max).then_inc(block_maxed, 1)
                            dve.wait_ge(block_maxed, first + 1)
                            nc.vector.tensor_tensor(child_max[:], child_max[:], block_max[:], ALU.max) \
                                .then_inc(block_used, 1)
                            wait_apart(dve, block_used, done + 2)
                            dve.reg_add(blocks, blocks, 1)
                            dve.reg_add(maxed, maxed, 1)

                        nc.vector.tensor_tensor(redo_max[:], child_max[:], redo_parent[:], ALU.add) \
                            .then_inc(redo_max_step, 1)
                        dve.wait_ge(redo_max_step, again * 3 + 1)
                        nc.vector.scalar_tensor_tensor(redo_max[:], redo_max[:], ALPHA, redo_max[:], ALU.mult, ALU.max) \
                            .then_inc(redo_max_step, 1)
                        dve.wait_ge(redo_max_step, again * 3 + 2)
                        nc.vector.tensor_scalar(redo_max[:], redo_max[:], FLOOR, None, ALU.max) \
                            .then_inc(redo_max_step, 1)
                        wait_apart(dve, redo_max_step, again * 3 + 3)

                        with dve.Fori(0, TILES):
                            done = dve.snap(blocks, min_val=0, max_val=2 * TILES * TILES)
                            second = dve.snap(rounds, min_val=0, max_val=TILES * TILES)
                            mark_edges(done)
                            nc.vector.tensor_tensor(logits_block, spread_child, over_columns(redo_parent[:]), ALU.add) \
                                .then_inc(pair_added, 1)
                            dve.wait_ge(pair_added, second + 1)
                            nc.vector.scalar_tensor_tensor(logits_block, logits_block, ALPHA, logits_block, ALU.mult,
                                                           ALU.max).then_inc(pair_leaky, 1)
                            dve.wait_ge(pair_leaky, second + 1)
                            nc.vector.tensor_tensor(logits_block, logits_block, over_columns(redo_max[:]),
                                                    ALU.subtract).then_inc(pair_shifted, 1)
                            dve.wait_ge(pair_shifted, second + 1)
                            dve.wait_ge(edges_marked, done + 1)
                            nc.vector.scalar_tensor_tensor(logits_block, off_edges(), FAR, logits_block, ALU.mult,
                                                           ALU.add).then_inc(pair_masked, 1)
                            dve.wait_ge(pair_exp, second + 1)
                            nc.vector.tensor_reduce(block_sum[:], shares_block, AX_X, ALU.add).then_inc(pair_summed, 1)
                            dve.wait_ge(pair_turned, second + 1)
                            nc.vector.tensor_copy(turned_block, summed[1][:].rearrange("p (h j) -> p h j", h=H)) \
                                .then_inc(pair_copied, 1)
                            dve.wait_ge(pair_summed, second + 1)
                            nc.vector.tensor_tensor(redo_sum[:], redo_sum[:], block_sum[:], ALU.add)
                            dve.wait_ge(pair_applied, second + 1)
                            nc.vector.tensor_tensor(redo_acc[:].rearrange("p h f -> p (h f)"),
                                                    redo_acc[:].rearrange("p h f -> p (h f)"), small[0][:, 0:D],
                                                    ALU.add).then_inc(block_used, 1)
                            wait_apart(dve, block_used, done + 2)
                            dve.reg_add(blocks, blocks, 1)
                            dve.reg_add(rounds, rounds, 1)

                        nc.vector.tensor_scalar(redo_lone[:], redo_sum[:, 0:1], 0.0, None, ALU.is_le) \
                            .then_inc(redo_end_step, 1)
                        dve.wait_ge(redo_end_step, again * 4 + 1)
                        nc.vector.tensor_scalar(redo_sum[:], redo_sum[:], redo_lone[:], None, ALU.add)
                        nc.vector.scalar_tensor_tensor(redo_acc[:].rearrange("p h f -> p (h f)"), mean_all[:, 0:D],
                                                       redo_lone[:], redo_acc[:].rearrange("p h f -> p (h f)"),
                                                       ALU.mult, ALU.add).then_inc(redo_end_step, 1)
                        dve.wait_ge(redo_end_step, again * 4 + 2)
                        nc.vector.reciprocal(redo_inv[:], redo_sum[:]).then_inc(redo_end_step, 1)
                        dve.wait_ge(redo_end_step, again * 4 + 3)
                        nc.vector.tensor_tensor(redo_acc[:], redo_acc[:],
                                                redo_inv[:].unsqueeze(2).to_broadcast([P, H, DH]), ALU.mult) \
                            .then_inc(redo_end_step, 1)
                        dve.wait_ge(redo_end_step, again * 4 + 4)
                        nc.vector.tensor_tensor(redo_out.unsqueeze(1),
                                                redo_acc[:].rearrange("p h f -> p (h f)").unsqueeze(1),
                                                x_all[:, one(t), :], ALU.add).then_inc(redo_staged, 1)
                        wait_apart(dve, redo_staged, again + 1)
                        dve.reg_add(redone, redone, 1)
                    with dve.Else():
                        dve.nop()
                    dve.nop()
                dve.nop()
            with dve.Else():
                dve.nop()
            dve.nop()

        @block.tensor
        def _(pe):
            def turn_group(g, u):
                pe.wait_ge(vector_normed, g + 1)
                pe.wait_ge(scalar_normed, g + 1)
                wait(pe, group_relu, g - 1)
                for a in range(GROUP):
                    done = nc.tensor.transpose(summed[u][:, a * P:(a + 1) * P], normed[u][:, a, :], eye[:])
                done.then_inc(group_turned, 1)

            def project_group(g, u):
                pe.wait_ge(group_relu, g + 1)
                wait(pe, group_staged, g - 1)
                for a in range(GROUP):
                    done = nc.tensor.matmul(projected(u)[:, a // 2, a % 2, :], h_turned[u][:, a, :], w_aug[:],
                                            start=True, stop=True)
                done.then_inc(group_projected, 1)

            def group_pair(i):
                turn_group(2 * i + 1, 1)
                project_group(2 * i, 0)
                turn_group(2 * i + 2, 0)
                project_group(2 * i + 1, 1)

            pe.wait_ge(eye_made, 1)
            pe.wait_ge(w_aug_made, 1)
            turn_group(0, 0)
            group_pair(0)
            with pe.Fori(1, GROUPS // 2 - 1) as i:
                group_pair(i)
            turn_group(GROUPS - 1, 1)
            for u in range(2):
                project_group(GROUPS - 2 + u, u)
            pe.wait_ge(h_mean_made, 1)
            nc.tensor.matmul(small[0][0:1, 0:ROW], h_mean[:], w_aug[:, 0:ROW], start=True, stop=True) \
                .then_inc(mean_projected, 1)

            def pack(t, b):
                wait(pe, words_read, t - 1)
                for h in range(WORDS // BANK):
                    nc.tensor.matmul(words[b][:, h * BANK:(h + 1) * BANK], pos_weight[:],
                                     pos_row[:, h * BANK:(h + 1) * BANK], start=True, stop=False)
                for q in range(CHUNKS):
                    pe.wait_ge(chunk_converted, t * CHUNKS + q + 1)
                    for k in range(PER_CHUNK):
                        c = q * PER_CHUNK + k
                        for h in range(WORDS // BANK):
                            at = c * WORDS + h * BANK
                            done = nc.tensor.matmul(words[b][:, h * BANK:(h + 1) * BANK], eye_bits[:, c, :],
                                                    edge[b][:, at:at + BANK], start=False, stop=(c == BITS - 1))
                done.then_inc(words_packed, 1)

            def turn_count(t, b):
                pe.wait_ge(used_counted, t + 1)
                wait(pe, most_ready, t - 1)
                nc.tensor.matmul(small[b][0:1, 0:P], n_used[b][:], eye[:], start=True, stop=True) \
                    .then_inc(count_turned, 1)

            def add_up(t, b):
                wait(pe, out_staged, t - 1)
                nc.tensor.matmul(summed[b][:, 0:D], eye[:], x_all[:, one(t), :].squeeze(1), start=True, stop=False)
                for half, of in enumerate(HALVES):
                    pe.wait_ge(product_made, 2 * t + half + 1)
                    for s in range(of.start, of.stop):
                        done = nc.tensor.matmul(summed[b][:, 0:D], eye[:], product[b][:, s, :], start=False,
                                                stop=(s == SLOTS - 1))
                done.then_inc(tile_summed, 1)

            def step(i, r):
                t, k, _ = at(i, r, 1)
                if is_tile(t):
                    turn_count(t, k % 2)
                t, k, _ = at(i, r)
                if is_tile(t):
                    pack(t, k % 2)
                t, k, _ = at(i, r, LAG)
                if is_tile(t):
                    add_up(t, k % 2)

            pe.wait_ge(masks_made, 3)
            pe.wait_ge(pos_made, 2)
            pe.wait_ge(eye_bits_made, 1)
            pe.wait_ge(group_staged, GROUPS)
            pe.wait_ge(mean_staged, 1)
            every_step(pe, step)

            pe.wait_ge(short_made, 1)
            pe.wait_ge(most_ready, TILES)
            nc.tensor.matmul(small[0][0:1, 0:TILES], ones_col[:], short[:], start=True, stop=True) \
                .then_inc(short_turned, 1)

            pe.wait_ge(flags_made, 2)
            pe.wait_ge(out_staged, TILES)
            some = pe.value_load(any_flag[0:1, 0:1], min_val=0, max_val=P)
            blocks = pe.alloc_register("blocks_seen")
            rounds = pe.alloc_register("blocks_applied")
            pe.reg_mov(blocks, 0)
            pe.reg_mov(rounds, 0)

            def spread(done):
                pe.wait_ge(block_landed, done * 32 + 32)
                for h in range(H):
                    last = nc.tensor.matmul(summed[0][:, h * P:(h + 1) * P],
                                            table_block[:, D + h:D + h + 1].to_broadcast([P, P]), eye[:],
                                            start=True, stop=True)
                last.then_inc(child_spread, 1)

            with pe.If(some > 0):
                with pe.Fori(0, TILES) as t:
                    flag = pe.value_load(flags[0:1, one(t)], min_val=0, max_val=P)
                    with pe.If(flag > 0):
                        with pe.Fori(0, TILES):
                            spread(pe.snap(blocks, min_val=0, max_val=2 * TILES * TILES))
                            pe.reg_add(blocks, blocks, 1)
                        with pe.Fori(0, TILES):
                            spread(pe.snap(blocks, min_val=0, max_val=2 * TILES * TILES))
                            second = pe.snap(rounds, min_val=0, max_val=TILES * TILES)
                            pe.wait_ge(pair_exp, second + 1)
                            for h in range(H):
                                last = nc.tensor.transpose(summed[1][:, h * P:(h + 1) * P], shares_block[:, h, :],
                                                           eye[:])
                            last.then_inc(pair_turned, 1)
                            pe.wait_ge(pair_copied, second + 1)
                            for h in range(H):
                                last = nc.tensor.matmul(small[0][:, h * DH:(h + 1) * DH], turned_block[:, h, :],
                                                        table_block[:, h * DH:(h + 1) * DH], start=True, stop=True)
                            last.then_inc(pair_applied, 1)
                            pe.reg_add(blocks, blocks, 1)
                            pe.reg_add(rounds, rounds, 1)
                        pe.nop()
                    with pe.Else():
                        pe.nop()
                    pe.nop()
                pe.nop()
            with pe.Else():
                pe.nop()
            pe.nop()


_INS = ["x", "adj", "L0_gnn_weight", "L0_gnn_att_weight"]
_OUT = ((8192, 128), "float32")


def kernel(**inputs):
    import numpy as _np
    import concourse.bacc as _bacc
    from concourse import mybir as _mybir
    from concourse.bass_utils import run_bass_kernel_spmd as _run

    nc = _bacc.Bacc("TRN2", target_bir_lowering=False, num_devices=1)
    arrays, args = {}, []
    for name in _INS:
        a = _np.ascontiguousarray(inputs[name])
        arrays[f"in_{name}_dram"] = a
        args.append(nc.dram_tensor(f"in_{name}_dram", a.shape, _mybir.dt.from_np(a.dtype), kind="ExternalInput").ap())
    shape, dtype = _OUT
    args.append(nc.dram_tensor("out_0_dram", shape, _mybir.dt.from_np(_np.dtype(dtype)), kind="ExternalOutput").ap())
    gat_kernel(nc, *args)
    r = _run(nc, [arrays], core_ids=[0])
    return r.results[0]["out_0_dram"]
```
